# Optimizing a Trainium2 kernel written in Bass

```python
import numpy as np
import jax
import jax.numpy as jnp

def _softmax(x, axis=-1):
    return jax.nn.softmax(x, axis=axis)

def _gelu(x):
    return jax.nn.gelu(x, approximate=True)

def _silu(x):
    return jax.nn.silu(x)

def _sigmoid(x):
    return jax.nn.sigmoid(x)

def _layernorm(x, axis=-1, eps=1e-05):
    m = jnp.mean(x, axis=axis, keepdims=True)
    v = jnp.var(x, axis=axis, keepdims=True)
    return (x - m) / jnp.sqrt(v + eps)

def _scatter_add(tgt, idx, src, axis=0):
    return tgt.at[idx].add(src)

def _segment_sum(src, seg, n):
    return jax.ops.segment_sum(src, seg, n)
kernel_name = 'mk_gnn_preln_d2_gnn_r8_45853c'

def setup_inputs(seed: int=0):
    np.random.seed(seed)
    _w = jnp.asarray

    def _rec_inputs():
        import jax
        import jax.numpy as jnp
        _gk = jax.random.key(seed)
        x = -0.0005121 + 1.001 * jax.random.normal(jax.random.fold_in(_gk, 1), (6250, 64), jnp.float32)
        src = jax.random.randint(jax.random.fold_in(_gk, 2), (200000,), 0, 6250, jnp.int32)
        dst = jnp.minimum((6250 * jax.random.uniform(jax.random.fold_in(_gk, 3), (200000,)) ** 2.0).astype(jnp.int32), 49999)
        _o = jnp.argsort(dst, stable=True)
        src = src[_o]
        dst = dst[_o]
        edge_attr_64 = -8.16379e-05 + 0.999858 * jax.random.normal(jax.random.fold_in(_gk, 12), (200000, 64), jnp.float32)
        return (x, src, dst, edge_attr_64)
    x, src, dst, edge_attr_64 = _rec_inputs()

    def _L0_gnn_setup():
        import jax, jax.numpy as jnp
        import numpy as np
        N = 6250
        E = 100000
        DIN = 64
        DEMB = 64
        H = 4
        DH = DEMB // H
        DFFN = DIN
        SLOPE = 0.2
        key = jax.random.key(seed)
        ks = jax.random.split(key, 9)
        s = 0.05
        return {'node_attr': jax.random.normal(ks[0], (N, DIN), jnp.float32), 'edge_index': jax.random.randint(ks[1], (E, 2), 0, N, dtype=jnp.int32), 'Wl': jax.random.normal(ks[2], (DEMB, DIN), jnp.float32) * s, 'Wr': jax.random.normal(ks[3], (DEMB, DIN), jnp.float32) * s, 'att': jax.random.normal(ks[4], (1, H, DH), jnp.float32) * s, 'W1': jax.random.normal(ks[5], (DFFN, DEMB + DIN), jnp.float32) * s, 'b1': jnp.zeros((DFFN,), jnp.float32), 'W2': jax.random.normal(ks[6], (DEMB, DFFN), jnp.float32) * s, 'b2': jnp.zeros((DEMB,), jnp.float32)}
    _L0_gnn_all = _L0_gnn_setup()
    _L0_gnn_in = {k: v for k, v in _L0_gnn_all.items() if k in ('Wl', 'Wr', 'att', 'W1', 'b1', 'W2', 'b2')}
    del _L0_gnn_all

    def _L1_gnn_setup():
        import jax, jax.numpy as jnp
        import numpy as np
        N_NODES = 12500
        N_EDGES = 200000
        EMB = 64
        BN_EPS = 1e-05
        key = jax.random.key(seed)
        ks = jax.random.split(key, 8)
        node_feats = jax.random.normal(ks[0], (N_NODES, EMB), dtype=jnp.float32)
        edge_feats = jax.random.normal(ks[1], (N_EDGES, EMB), dtype=jnp.float32)
        src = jax.random.randint(ks[2], (N_EDGES,), 0, N_NODES, dtype=jnp.int32)
        dst = jax.random.randint(ks[3], (N_EDGES,), 0, N_NODES, dtype=jnp.int32)
        lim1 = 1.0 / np.sqrt(EMB)
        lim2 = 1.0 / np.sqrt(2 * EMB)
        W1 = jax.random.uniform(ks[4], (EMB, 2 * EMB), minval=-lim1, maxval=lim1, dtype=jnp.float32)
        b1 = jax.random.uniform(ks[5], (2 * EMB,), minval=-lim1, maxval=lim1, dtype=jnp.float32)
        W2 = jax.random.uniform(ks[6], (2 * EMB, EMB), minval=-lim2, maxval=lim2, dtype=jnp.float32)
        b2 = jax.random.uniform(ks[7], (EMB,), minval=-lim2, maxval=lim2, dtype=jnp.float32)
        bn_gamma = jnp.ones((EMB,), dtype=jnp.float32)
        bn_beta = jnp.zeros((EMB,), dtype=jnp.float32)
        return {'node_feats': node_feats, 'edge_feats': edge_feats, 'src': src, 'dst': dst, 'W1': W1, 'b1': b1, 'W2': W2, 'b2': b2, 'bn_gamma': bn_gamma, 'bn_beta': bn_beta}
    _L1_gnn_all = _L1_gnn_setup()
    _L1_gnn_in = {k: v for k, v in _L1_gnn_all.items() if k in ('W1', 'b1', 'W2', 'b2', 'bn_gamma', 'bn_beta')}
    del _L1_gnn_all
    return {'x': x, 'src': src, 'dst': dst, 'edge_attr_64': edge_attr_64, 'L0_gnn_Wl': _L0_gnn_in['Wl'], 'L0_gnn_Wr': _L0_gnn_in['Wr'], 'L0_gnn_att': _L0_gnn_in['att'], 'L0_gnn_W1': _L0_gnn_in['W1'], 'L0_gnn_b1': _L0_gnn_in['b1'], 'L0_gnn_W2': _L0_gnn_in['W2'], 'L0_gnn_b2': _L0_gnn_in['b2'], 'L1_gnn_W1': _L1_gnn_in['W1'], 'L1_gnn_b1': _L1_gnn_in['b1'], 'L1_gnn_W2': _L1_gnn_in['W2'], 'L1_gnn_b2': _L1_gnn_in['b2'], 'L1_gnn_bn_gamma': _L1_gnn_in['bn_gamma'], 'L1_gnn_bn_beta': _L1_gnn_in['bn_beta']}

def reference(x, src, dst, edge_attr_64, L0_gnn_Wl, L0_gnn_Wr, L0_gnn_att, L0_gnn_W1, L0_gnn_b1, L0_gnn_W2, L0_gnn_b2, L1_gnn_W1, L1_gnn_b1, L1_gnn_W2, L1_gnn_b2, L1_gnn_bn_gamma, L1_gnn_bn_beta):
    import jax
    import jax.numpy as jnp

    def _L0_gnn_ref(node_attr, edge_index, Wl, Wr, att, W1, b1, W2, b2):
        import jax, jax.numpy as jnp
        import numpy as np
        N = 6250
        E = 100000
        DIN = 64
        DEMB = 64
        H = 4
        DH = DEMB // H
        DFFN = DIN
        SLOPE = 0.2
        ngl = (node_attr @ Wl.T).reshape(N, H, DH)
        ngr = (node_attr @ Wr.T).reshape(N, H, DH)
        idx = jnp.concatenate([edge_index, edge_index[:, ::-1]], axis=0)
        src, dst = (idx[:, 0], idx[:, 1])
        gl = ngl[src]
        gr = ngr[dst]
        score = (att * jax.nn.leaky_relu(gl + gr, SLOPE)).sum(-1)
        m = jax.ops.segment_max(score, src, num_segments=N)
        ex = jnp.exp(score - m[src])
        denom = jax.ops.segment_sum(ex, src, num_segments=N)
        alpha = ex / (denom[src] + 1e-16)
        out = jax.ops.segment_sum(gr * alpha[:, :, None], src, num_segments=N)
        out = out.reshape(N, H * DH)
        h = jnp.concatenate([out, node_attr], axis=1)
        h = jax.nn.gelu(h @ W1.T + b1, approximate=False)
        return h @ W2.T + b2

    def _L1_gnn_ref(node_feats, edge_feats, src, dst, W1, b1, W2, b2, bn_gamma, bn_beta):
        import jax, jax.numpy as jnp
        import numpy as np
        N_NODES = 12500
        N_EDGES = 200000
        EMB = 64
        BN_EPS = 1e-05
        n_nodes = node_feats.shape[0]
        msg = node_feats[src] + edge_feats
        agg = jax.ops.segment_sum(msg, dst, num_segments=n_nodes)
        h = jax.nn.relu(agg @ W1 + b1) @ W2 + b2
        mean = jnp.mean(h, axis=0)
        var = jnp.mean(jnp.square(h - mean), axis=0)
        h = (h - mean) * jax.lax.rsqrt(var + BN_EPS) * bn_gamma + bn_beta
        return h
    edge_index_t = jnp.stack([src, dst], axis=1)
    h = jnp.maximum(_layernorm(x, axis=-1), 0.0)
    x = x + _L0_gnn_ref(h, edge_index_t, L0_gnn_Wl, L0_gnn_Wr, L0_gnn_att, L0_gnn_W1, L0_gnn_b1, L0_gnn_W2, L0_gnn_b2)
    h = jnp.maximum(_layernorm(x, axis=-1), 0.0)
    x = x + _L1_gnn_ref(h, edge_attr_64, src, dst, L1_gnn_W1, L1_gnn_b1, L1_gnn_W2, L1_gnn_b2, L1_gnn_bn_gamma, L1_gnn_bn_beta)
    return x

_drawn_inputs = setup_inputs


def setup_inputs(seed=0):
    import zlib

    import numpy as np

    out = dict(_drawn_inputs(seed))
    spreads = {'L0_gnn_b1': (0.0, 0.1),
     'L0_gnn_b2': (0.0, 0.1),
     'L1_gnn_bn_gamma': (1.0, 0.2),
     'L1_gnn_bn_beta': (0.0, 0.1)}
    factors = {'L0_gnn_Wl': 64.0,
     'L0_gnn_Wr': 2.783,
     'L0_gnn_att': 34.984,
     'L1_gnn_b1': 8.0,
     'L1_gnn_b2': 64.0}
    for name, (base, spread) in spreads.items():
        noise = np.random.default_rng([zlib.crc32(name.encode()), seed]).standard_normal(out[name].shape)
        drawn = base * np.exp(spread * noise) if base else spread * noise
        out[name] = jnp.asarray(drawn.astype(out[name].dtype))
    for name, factor in factors.items():
        out[name] = (out[name] * factor).astype(out[name].dtype)
    return out
```

```python
from contextlib import ExitStack

import numpy as np

import concourse.bass as bass
from concourse import mybir

F32 = mybir.dt.float32
BF16 = mybir.dt.bfloat16
I32 = mybir.dt.int32
ALU = mybir.AluOpType
ACT = mybir.ActivationFunctionType
AX = mybir.AxisListType

P = 128
N, E, D = 6250, 200000, 64
HEADS = 4
DH = D // HEADS
SLOPE = 0.2
LN_EPS = 1e-5
BN_EPS = 1e-5
BLOCKS = -(-N // P)
LAST = N - (BLOCKS - 1) * P

EDGE_TILES = 8
EDGE_GROUP = EDGE_TILES * P
EDGE_GROUPS = -(-E // EDGE_GROUP)
FULL_EDGES = (EDGE_GROUPS - 1) * EDGE_GROUP
TAIL_PARTS = (E - FULL_EDGES) // EDGE_TILES
EDGE_COLS = EDGE_GROUPS * EDGE_TILES
FULL_COLS = EDGE_COLS - EDGE_TILES

GROUP_TILES = 4
GROUP = GROUP_TILES * P
LOG_P, LOG_ROW = 7, 12
ROW = 1 << LOG_ROW
SORT_LOG = LOG_P + LOG_ROW
NODE_BITS = 13
NODE_MASK = (1 << NODE_BITS) - 1
KEY_BIT = 1 << (2 * NODE_BITS + 1)
NO_KEY = float(np.array([KEY_BIT | ((1 << 2 * NODE_BITS) - 1)], np.int32).view(np.float32)[0])
CHUNKS = 4
CHUNK_ROWS = 32
GROUPS = 832
assert GROUPS * GROUP >= 2 * E + BLOCKS * (GROUP - 1) and GROUPS * GROUP <= 1 << SORT_LOG
TILES = GROUPS * GROUP_TILES
CHUNK_GROUPS = GROUPS // CHUNKS
CHUNK_TILES = TILES // CHUNKS
ROW_TILES = CHUNK_TILES // CHUNK_ROWS
SCAN = ROW_TILES * P
PAD = 8 * GROUP_TILES
FAR = 8192.0
BIG = 1e30
ACCW = DH + 1
SHIFT = 16384


def at_least(eng, sem, value):
    if isinstance(value, int) and value <= 0:
        return
    eng.wait_ge(sem, value)


def load_blocks(eng, tile, dram, sem):
    full = (BLOCKS - 1) * P
    eng.dma_start(tile[:, 0:BLOCKS - 1, :], dram[0:full, :].rearrange("(b p) f -> p b f", p=P)).then_inc(sem, 16)
    eng.dma_start(tile[0:LAST, BLOCKS - 1, :], dram[full:N, :]).then_inc(sem, 16)


def store_blocks(eng, dram, tile, sem):
    full = (BLOCKS - 1) * P
    eng.dma_start(dram[0:full, :].rearrange("(b p) f -> p b f", p=P), tile[:, 0:BLOCKS - 1, :]).then_inc(sem, 16)
    eng.dma_start(dram[full:N, :], tile[0:LAST, BLOCKS - 1, :]).then_inc(sem, 16)


class Chain:

    def __init__(self, eng, sem):
        self.eng, self.sem, self.n = eng, sem, 0

    def link(self, ins):
        self.n += 1
        ins.then_inc(self.sem, 1)
        self.eng.wait_ge(self.sem, self.n)



class Memory:
    pass


def layernorm_steps(m, chain, dve, x, h, square, s_var, s_std, turn):
    chain.link(nc_reduce(dve, m.mean[:, :], x[:, :, :]))
    chain.link(dve.tensor_scalar(m.mean[:, :], m.mean[:, :], 1.0 / D, None, ALU.mult))
    spread = m.mean[:, :].unsqueeze(2).to_broadcast([P, BLOCKS, D])
    chain.link(dve.tensor_tensor(h[:, :, :], x[:, :, :], spread, ALU.subtract))
    chain.link(dve.tensor_tensor(square[:, :, :], h[:, :, :], h[:, :, :], ALU.mult))
    chain.link(nc_reduce(dve, m.var[:, :], square[:, :, :]))
    dve.tensor_scalar(m.var[:, :], m.var[:, :], 1.0 / D, LN_EPS, ALU.mult, ALU.add).then_inc(s_var, 1)
    dve.wait_ge(s_std, turn)
    chain.link(dve.reciprocal(m.rstd[:, :], m.rstd[:, :]))
    chain.link(dve.tensor_tensor(m.mean[:, :], m.rstd[:, :], m.rstd[:, :], ALU.mult))
    chain.link(dve.tensor_tensor(m.mean[:, :], m.mean[:, :], m.var[:, :], ALU.mult))
    chain.link(dve.tensor_scalar(m.mean[:, :], m.mean[:, :], -0.5, 1.5, ALU.mult, ALU.add))
    chain.link(dve.tensor_tensor(m.rstd[:, :], m.rstd[:, :], m.mean[:, :], ALU.mult))
    spread = m.rstd[:, :].unsqueeze(2).to_broadcast([P, BLOCKS, D])
    return dve.scalar_tensor_tensor(h[:, :, :], h[:, :, :], 0.0, spread, ALU.max, ALU.mult)


def nc_reduce(dve, out, in_, op=ALU.add):
    return dve.tensor_reduce(out, in_, AX.X, op)


def build(nc, t, out, stop=None):
    with ExitStack() as whole:
        m = Memory()
        m.nc, m.t, m.out = nc, t, out

        def sb(name, shape, dt, ctx=whole):
            return ctx.enter_context(nc.sbuf_tensor(name, shape, dt))

        def sem(name):
            return whole.enter_context(nc.semaphore(name))

        m.sb, m.sem = sb, sem
        m.bank = [whole.enter_context(nc.psum_tensor(f"bank{i}", [P, 512], F32)) for i in range(8)]

        m.gr_table = nc.dram_tensor("gr_table", (N, D), F32).ap()
        m.h2_table = nc.dram_tensor("h2_table", (N, D), F32).ap()
        m.gr_rows = nc.dram_tensor("gr_rows", (GROUPS, P, GROUP_TILES * D), F32).ap()

        m.h = sb("h_sb", [P, BLOCKS, D], F32)
        m.src = sb("src_sb", [P, EDGE_COLS], I32)
        m.dst = sb("dst_sb", [P, EDGE_COLS], I32)
        m.ident = sb("ident", [P, P], F32)
        m.ident_bf = sb("ident_bf", [P, P], BF16)
        m.ones = sb("ones", [P, P], F32)
        m.iota_row = sb("iota_row", [P, P], F32)
        m.iota_node = sb("iota_node", [P, BLOCKS], F32)
        m.att = sb("att_sb", [P, D], F32)
        m.w1t_out = sb("w1t_out", [D, D], F32)
        m.w1t_h = sb("w1t_h", [D, D], F32)
        m.b1_l0 = sb("b1_l0", [D, 1], F32)
        m.w2t = sb("w2t", [D, D], F32)
        m.b2_l0 = sb("b2_l0", [P, D], F32)
        m.w1_l1 = sb("w1_l1", [D, 2 * D], F32)
        m.b1_l1 = sb("b1_l1", [2 * D, 1], F32)
        m.w2_l1 = sb("w2_l1", [2 * D, D], F32)
        m.cols_l1 = sb("cols_l1", [D, 3], F32)
        m.mean = sb("mean", [P, BLOCKS], F32)
        m.var = sb("var", [P, BLOCKS], F32)
        m.rstd = sb("rstd", [P, BLOCKS], F32)
        m.blk_i = sb("blk_i", [1, GROUPS + 1], I32)
        m.blk_f = sb("blk_f", [1, GROUPS], F32)

        m.acc = sb("acc", [P, BLOCKS, HEADS * ACCW], F32)
        layer0, keys_ctx = (whole.enter_context(ExitStack()) for _ in range(2))
        m.gl_parts = sb("gl_parts", [P, BLOCKS, 3 * D], BF16, layer0)
        m.place = sb("place", [P, TILES + PAD], F32, layer0)
        m.row_of = sb("row_of", [P, TILES + PAD], I32, layer0)
        m.pen = sb("pen", [P, TILES], BF16, layer0)

        m.keys = [sb("keys0", [P, ROW], F32, keys_ctx), sb("keys1", [P, ROW], F32, keys_ctx)]
        with ExitStack() as ctx:
            prepare(m, ctx)
        if stop == "prepare":
            return m
        with ExitStack() as ctx:
            final = sort(m, ctx)
        if stop == "sort":
            return m
        with ExitStack() as ctx:
            decode(m, ctx, final)
        keys_ctx.close()
        if stop == "decode":
            return m
        with ExitStack() as ctx:
            attention(m, ctx)
        layer0.close()
        if stop == "attention":
            return m
        m.x = sb("x_sb", [P, BLOCKS, D], F32)
        with ExitStack() as ctx:
            attention_nodes(m, ctx)
        if stop == "nodes0":
            return m
        m.agg = sb("agg", [P, BLOCKS, D], F32)
        with ExitStack() as ctx:
            messages(m, ctx)
        with ExitStack() as ctx:
            message_nodes(m, ctx)
        return m


def prepare(m, ctx):
    nc, t, sb, sem, bank = m.nc, m.t, m.sb, m.sem, m.bank
    m.x = sb("x_in", [P, BLOCKS, D], F32, ctx)
    w_l0 = sb("w_l0", [D, 2, D], F32, ctx)
    w1_l0 = sb("w1_l0", [D, 2 * D], F32, ctx)
    w2_l0 = sb("w2_l0", [D, D], F32, ctx)
    w_lr_t = sb("w_lr_t", [D, 2 * D], F32, ctx)
    ht = [sb(f"ht{i}", [D, 4 * P], F32, ctx) for i in range(2)]
    gl = sb("gl", [P, BLOCKS, D], F32, ctx)
    gr = sb("gr", [P, BLOCKS, D], F32, ctx)
    src_f = sb("src_f", [P, 2 * EDGE_COLS], F32, ctx)
    below = sb("below", [P, BLOCKS], F32, ctx)
    counts = sb("counts", [P, BLOCKS], F32, ctx)
    room = sb("room", [P, BLOCKS], I32, ctx)
    room_f = sb("room_f", [P, BLOCKS], F32, ctx)
    ends = sb("ends", [P, BLOCKS], F32, ctx)
    end_col = sb("end_col", [BLOCKS, 1], F32, ctx)
    iota_group = sb("iota_group", [BLOCKS, GROUPS], F32, ctx)
    past = sb("past", [BLOCKS, GROUPS], F32, ctx)
    ordinal = sb("ordinal", [P, GROUP_TILES], F32, ctx)
    pad_key = sb("pad_key", [P, BLOCKS], I32, ctx)
    unused = sb("unused", [P, BLOCKS, GROUP_TILES], I32, ctx)
    junk = sb("junk", [P, 2 * EDGE_COLS], BF16, ctx)

    s_init = sem("s_init")
    s_edges = sem("s_edges")
    s_x = sem("s_x")
    s_weights = sem("s_weights")
    s_const = sem("s_const")
    s_ident = sem("s_ident")
    s_var0, s_std0 = sem("s_var0"), sem("s_std0")
    s_h = sem("s_h")
    s_wt_ps, s_wt = sem("s_wt_ps"), sem("s_wt")
    s_ht_ps, s_ht = sem("s_ht_ps"), sem("s_ht")
    s_lr_ps = sem("s_lr_ps")
    s_lr = sem("s_lr")
    s_grt = sem("s_grt")
    s_cnt, s_cnt_ps = sem("s_cnt"), sem("s_cnt_ps")
    s_end, s_end_ps = sem("s_end"), sem("s_end_ps")
    s_past, s_past_ps = sem("s_past"), sem("s_past_ps")
    s_chain = sem("s_prep_dve")

    rounds = [(b, min(4, BLOCKS - b)) for b in range(0, BLOCKS, 4)]
    w_count = 12

    with nc.Block() as block:
        @block.sync
        def _(sp):
            sp.wait_ge(s_init, 1)
            for dram, tile in ((t["src"], m.src), (t["dst"], m.dst)):
                sp.dma_start(tile[:, 0:FULL_COLS].rearrange("p (g t) -> p g t", t=EDGE_TILES),
                             dram[0:FULL_EDGES].rearrange("(g p t) -> p g t", p=P, t=EDGE_TILES)).then_inc(s_edges, 16)
                sp.dma_start(tile[0:TAIL_PARTS, FULL_COLS:EDGE_COLS],
                             dram[FULL_EDGES:E].rearrange("(p t) -> p t", t=EDGE_TILES)).then_inc(s_edges, 16)
            load_blocks(sp, m.x, t["x"], s_x)
            sp.wait_ge(s_lr, len(rounds))
            store_blocks(sp, m.gr_table, gr, s_grt)
            sp.wait_ge(s_grt, 32)

        @block.scalar
        def _(act):
            for dram, tile in (
                (t["L0_gnn_Wl"], w_l0[:, 0, :]), (t["L0_gnn_Wr"], w_l0[:, 1, :]),
                (t["L0_gnn_W1"], w1_l0[:, :]), (t["L0_gnn_W2"], w2_l0[:, :]),
                (t["L0_gnn_att"].rearrange("a h d -> a (h d)").to_broadcast([P, D]), m.att[:, :]),
                (t["L0_gnn_b1"].unsqueeze(1), m.b1_l0[:, :]),
                (t["L0_gnn_b2"].unsqueeze(0).to_broadcast([P, D]), m.b2_l0[:, :]),
                (t["L1_gnn_W1"], m.w1_l1[:, :]), (t["L1_gnn_b1"].unsqueeze(1), m.b1_l1[:, :]),
                (t["L1_gnn_W2"], m.w2_l1[:, :]),
                (t["L1_gnn_b2"].unsqueeze(1), m.cols_l1[:, 0:1]),
                (t["L1_gnn_bn_gamma"].unsqueeze(1), m.cols_l1[:, 1:2]),
                (t["L1_gnn_bn_beta"].unsqueeze(1), m.cols_l1[:, 2:3]),
            ):
                act.dma_start(tile, dram).then_inc(s_weights, 16)
            act.wait_ge(s_var0, 1)
            nc.scalar.activation(m.rstd[:, :], m.var[:, :], ACT.Sqrt).then_inc(s_std0, 1)
            for r, (b, n) in enumerate(rounds):
                act.wait_ge(s_ht_ps, r + 1)
                if r >= 2:
                    act.wait_ge(s_lr_ps, r - 1)
                nc.scalar.copy(ht[r % 2][:, 0:n * P], bank[r % 2][0:D, 0:n * P]).then_inc(s_ht, 1)
                act.wait_ge(s_lr_ps, r + 1)
                terms = bank[2 + r % 2][:, 0:n * P].rearrange("p (b w f) -> p b w f", w=2, f=D)
                nc.scalar.copy(gl[:, b:b + n, :], terms[:, :, 0, :])
                nc.scalar.copy(gr[:, b:b + n, :], terms[:, :, 1, :]).then_inc(s_lr, 1)

        @block.gpsimd
        def _(pool):
            pool.memset(m.ident[:, :], 0.0).then_inc(s_ident, 1)
            pool.iota(m.iota_row[:, :], [[1, P]], base=0, channel_multiplier=0,
                      allow_small_or_imprecise_dtypes=True).then_inc(s_const, 1)
            pool.iota(m.iota_node[:, :], [[P, BLOCKS]], base=0, channel_multiplier=1,
                      allow_small_or_imprecise_dtypes=True).then_inc(s_const, 1)
            pool.iota(iota_group[:, :], [[1, GROUPS]], base=0, channel_multiplier=0,
                      allow_small_or_imprecise_dtypes=True).then_inc(s_const, 1)
            pool.iota(ordinal[:, :], [[P, GROUP_TILES]], base=0, channel_multiplier=1,
                      allow_small_or_imprecise_dtypes=True).then_inc(s_const, 1)
            pool.iota(pad_key[:, :], [[1, BLOCKS]], base=0, channel_multiplier=0).then_inc(s_const, 1)
            pool.wait_ge(s_ident, 1)
            pool.affine_select(out=m.ident[:, :], in_=m.ident[:, :], compare_op=ALU.not_equal, fill=1.0, base=0,
                               pattern=[[-1, P]], channel_multiplier=1).then_inc(s_ident, 1)
            pool.wait_ge(s_ident, 2)
            pool.tensor_copy(m.ident_bf[:, :], m.ident[:, :]).then_inc(s_const, 1)

        @block.tensor
        def _(pe):
            pe.wait_ge(s_weights, 16 * 13)
            pe.wait_ge(s_ident, 2)
            pieces = (w_l0[:, 0, :], w_l0[:, 1, :], w1_l0[:, 0:D], w1_l0[:, D:2 * D], w2_l0[:, :])
            for i, w in enumerate(pieces):
                last = pe.transpose(bank[4][0:D, i * D:(i + 1) * D], w, m.ident[0:D, 0:D])
            last.then_inc(s_wt_ps, 1)
            pe.wait_ge(s_h, 1)
            pe.wait_ge(s_wt, 1)
            for r, (b, n) in enumerate(rounds):
                if r >= 2:
                    pe.wait_ge(s_ht, r - 1)
                for i in range(n):
                    last = pe.transpose(bank[r % 2][0:D, i * P:(i + 1) * P], m.h[:, b + i, :], m.ident[:, :])
                last.then_inc(s_ht_ps, 1)
                pe.wait_ge(s_ht, r + 1)
                if r >= 2:
                    pe.wait_ge(s_lr, r - 1)
                for i in range(n):
                    last = pe.matmul(bank[2 + r % 2][:, i * P:(i + 1) * P], ht[r % 2][:, i * P:(i + 1) * P],
                                     w_lr_t[:, :], start=True, stop=True)
                last.then_inc(s_lr_ps, 1)
            pe.wait_ge(s_cnt, 1)
            pe.matmul(bank[5][:, 0:BLOCKS], m.ones[:, :], below[:, :], start=True, stop=True).then_inc(s_cnt_ps, 1)
            pe.wait_ge(s_end, 1)
            pe.transpose(bank[6][0:BLOCKS, 0:P], ends[:, :], m.ident[:, :]).then_inc(s_end_ps, 1)
            pe.wait_ge(s_past, 1)
            half = GROUPS // 2
            for i in range(2):
                last = pe.matmul(bank[6 + i][:, 0:half], m.ones[0:BLOCKS, :], past[:, i * half:(i + 1) * half],
                                 start=True, stop=True)
            last.then_inc(s_past_ps, 1)

        @block.vector
        def _(dve):
            c = Chain(dve, s_chain)
            dve.memset(m.x[:, BLOCKS - 1, :], 0.0)
            dve.memset(m.src[:, FULL_COLS:EDGE_COLS], 0)
            dve.memset(m.dst[:, FULL_COLS:EDGE_COLS], -1).then_inc(s_init, 1)
            dve.memset(src_f[:, :], FAR)
            dve.memset(m.keys[0][:, :], NO_KEY)
            c.link(dve.memset(m.ones[:, :], 1.0))
            dve.wait_ge(s_wt_ps, 1)
            c.link(dve.tensor_copy(w_lr_t[:, :], bank[4][0:D, 0:2 * D]))
            dve.tensor_copy(m.w1t_out[:, :], bank[4][0:D, 2 * D:3 * D])
            dve.tensor_copy(m.w1t_h[:, :], bank[4][0:D, 3 * D:4 * D])
            dve.tensor_copy(m.w2t[:, :], bank[4][0:D, 4 * D:5 * D]).then_inc(s_wt, 1)
            dve.wait_ge(s_x, 32)
            layernorm_steps(m, c, dve, m.x, m.h, gl, s_var0, s_std0, 1).then_inc(s_h, 1)

            dve.wait_ge(s_edges, 64)
            ends_of = (m.src, m.dst)
            for way in range(2):
                a, b = ends_of[way], ends_of[1 - way]
                base = way * EDGE_COLS
                for parts, lo, hi in ((P, 0, FULL_COLS), (TAIL_PARTS, FULL_COLS, EDGE_COLS)):
                    key = m.keys[0][0:parts, base + lo:base + hi].bitcast(I32)
                    c.link(dve.scalar_tensor_tensor(key, a[0:parts, lo:hi], NODE_BITS, b[0:parts, lo:hi],
                                                    ALU.logical_shift_left, ALU.bitwise_or))
                    c.link(dve.tensor_single_scalar(key, key, KEY_BIT, ALU.bitwise_or))
                    c.link(dve.tensor_copy(src_f[0:parts, base + lo:base + hi], a[0:parts, lo:hi]))
            for b in range(BLOCKS):
                c.link(dve.tensor_scalar(junk[:, :], src_f[:, :], float(P * (b + 1)), None, ALU.is_lt, ALU.add,
                                         accum_out=below[:, b:b + 1]))
            dve.engine_nop().then_inc(s_cnt, 1)
            dve.wait_ge(s_lr, len(rounds))
            for part in range(3):
                piece = m.gl_parts[:, :, part * D:(part + 1) * D]
                c.link(dve.tensor_copy(piece, gl[:, :, :]))
                if part < 2:
                    c.link(dve.tensor_tensor(gl[:, :, :], gl[:, :, :], piece, ALU.subtract))

            dve.wait_ge(s_cnt_ps, 1)
            c.link(dve.tensor_copy(counts[:, :], bank[5][:, 0:BLOCKS]))
            c.link(dve.tensor_copy(below[:, :], counts[:, :]))
            c.link(dve.tensor_tensor(counts[:, 1:BLOCKS], below[:, 1:BLOCKS], below[:, 0:BLOCKS - 1], ALU.subtract))
            c.link(dve.tensor_scalar(room[:, :], counts[:, :], -1.0, float(1 << SORT_LOG), ALU.mult, ALU.add))
            c.link(dve.tensor_single_scalar(room[:, :], room[:, :], GROUP - 1, ALU.bitwise_and))
            c.link(dve.tensor_copy(room_f[:, :], room[:, :]))
            c.link(dve.tensor_tensor(counts[:, :], counts[:, :], room_f[:, :], ALU.add))
            c.link(dve.tensor_scalar(counts[:, :], counts[:, :], 1.0 / GROUP, None, ALU.mult))
            dve.tensor_tensor_scan(ends[:, :], m.ones[:, 0:BLOCKS], counts[:, :], 0.0, ALU.mult,
                                   ALU.add).then_inc(s_end, 1)
            dve.wait_ge(s_const, 6)
            c.link(dve.tensor_scalar(pad_key[:, :], pad_key[:, :], LOG_P + NODE_BITS,
                                     KEY_BIT | ((1 << LOG_P + NODE_BITS) - 1), ALU.logical_shift_left, ALU.bitwise_or))
            c.link(dve.tensor_tensor(unused[:, :, :], ordinal[:, :].unsqueeze(1).to_broadcast([P, BLOCKS, GROUP_TILES]),
                                     room_f[:, :].unsqueeze(2).to_broadcast([P, BLOCKS, GROUP_TILES]), ALU.is_ge))
            c.link(dve.tensor_scalar(unused[:, :, :], unused[:, :, :], 31, 31, ALU.logical_shift_left,
                                     ALU.arith_shift_right))
            c.link(dve.tensor_single_scalar(unused[:, :, :], unused[:, :, :], (1 << 2 * NODE_BITS) - 1, ALU.bitwise_and))
            pads = m.keys[0][:, 2 * EDGE_COLS:2 * EDGE_COLS + BLOCKS * GROUP_TILES].bitcast(I32)
            c.link(dve.tensor_tensor(pads.rearrange("p (b i) -> p b i", i=GROUP_TILES), unused[:, :, :],
                                     pad_key[:, :].unsqueeze(2).to_broadcast([P, BLOCKS, GROUP_TILES]), ALU.bitwise_or))
            dve.wait_ge(s_end_ps, 1)
            c.link(dve.tensor_copy(end_col[:, :], bank[6][0:BLOCKS, 0:1]))
            dve.tensor_scalar(past[:, :], iota_group[:, :], end_col[:, 0:1], None, ALU.is_ge).then_inc(s_past, 1)
            dve.wait_ge(s_past_ps, 1)
            half = GROUPS // 2
            for i in range(2):
                c.link(dve.tensor_scalar(m.blk_f[:, i * half:(i + 1) * half], bank[6 + i][0:1, 0:half],
                                         float(BLOCKS - 1), None, ALU.min))
            dve.memset(m.blk_i[:, GROUPS:GROUPS + 1], 0)
            c.link(dve.tensor_copy(m.blk_i[:, 0:GROUPS], m.blk_f[:, :]))


def sort(m, ctx):
    nc, sb, sem, bank = m.nc, m.sb, m.sem, m.bank
    bits = sb("bits", [P, LOG_P], I32, ctx)
    sign = sb("sign", [P, LOG_P + 1], F32, ctx)
    turn = sb("turn", [P, LOG_P + 1], F32, ctx)
    s_num = sem("s_num")
    s_chain = sem("s_sort_dve")
    s_ready = sem("s_sort_ready")
    s_tr = sem("s_sort_tr")
    s_act = sem("s_sort_act")
    s_dve = sem("s_sort_moved")
    turns = 2 * LOG_P
    banks = ROW // 512

    held = []

    with nc.Block() as block:
        @block.gpsimd
        def _(pool):
            pool.iota(bits[:, :], [[0, LOG_P]], base=0, channel_multiplier=1).then_inc(s_num, 1)

        @block.vector
        def _(dve):
            c = Chain(dve, s_chain)
            at = 0

            def one_pass(distance, run=None):
                nonlocal at
                a, b = m.keys[at], m.keys[1 - at]
                if run is None or run == ROW:
                    va = a[:, :].rearrange("p (a two c) -> p two a c", two=2, c=distance)
                    vb = b[:, :].rearrange("p (a two c) -> p two a c", two=2, c=distance)
                    dve.tensor_tensor(vb[:, 0], va[:, 0], va[:, 1], ALU.min)
                    last = dve.tensor_tensor(vb[:, 1], va[:, 0], va[:, 1], ALU.max)
                else:
                    form = "p (a way b two c) -> p way two a b c"
                    sizes = dict(way=2, two=2, b=run // (2 * distance), c=distance)
                    va, vb = a[:, :].rearrange(form, **sizes), b[:, :].rearrange(form, **sizes)
                    for way, (low, high) in enumerate(((ALU.min, ALU.max), (ALU.max, ALU.min))):
                        dve.tensor_tensor(vb[:, way, 0], va[:, way, 0], va[:, way, 1], low)
                        last = dve.tensor_tensor(vb[:, way, 1], va[:, way, 0], va[:, way, 1], high)
                c.link(last)
                at = 1 - at

            def transpose_keys():
                nonlocal at
                n = len(held)
                held.append(at)
                dve.engine_nop().then_inc(s_ready, 1)
                for k in range(1, banks, 2):
                    dve.wait_ge(s_tr, n * banks + k + 1)
                    dve.tensor_copy(m.keys[1 - at][:, 512 * k:512 * (k + 1)], bank[k][:, :]).then_inc(s_dve, 1)
                dve.wait_ge(s_dve, (n + 1) * banks // 2)
                dve.wait_ge(s_act, (n + 1) * banks // 2)
                at = 1 - at

            dve.wait_ge(s_num, 1)
            for i in range(LOG_P):
                c.link(dve.tensor_scalar(bits[:, i:i + 1], bits[:, i:i + 1], i, 1, ALU.logical_shift_right,
                                         ALU.bitwise_and))
            c.link(dve.memset(sign[:, LOG_P:LOG_P + 1], 1.0))
            c.link(dve.tensor_scalar(sign[:, 0:LOG_P], bits[:, :], -2.0, 1.0, ALU.mult, ALU.add))
            c.link(dve.tensor_copy(turn[:, 0:1], sign[:, 0:1]))
            c.link(dve.tensor_tensor(turn[:, 1:LOG_P + 1], sign[:, 1:LOG_P + 1], sign[:, 0:LOG_P], ALU.mult))

            for stage in range(1, SORT_LOG + 1):
                if stage >= LOG_ROW:
                    which = stage - LOG_ROW
                    c.link(dve.tensor_scalar(m.keys[at][:, :], m.keys[at][:, :], turn[:, which:which + 1], None,
                                             ALU.mult))
                if stage > LOG_ROW:
                    transpose_keys()
                    for i in reversed(range(stage - LOG_ROW)):
                        one_pass(1 << i)
                    transpose_keys()
                for i in reversed(range(min(stage, LOG_ROW))):
                    one_pass(1 << i, 1 << stage if stage < LOG_ROW else None)
            m.sorted_in = at

        @block.tensor
        def _(pe):
            for n in range(turns):
                pe.wait_ge(s_ready, n + 1)
                for k in range(banks):
                    for i in range(4):
                        j = 4 * k + i
                        last = pe.transpose(bank[k][:, i * P:(i + 1) * P], m.keys[held[n]][:, j * P:(j + 1) * P],
                                            m.ident[:, :])
                    last.then_inc(s_tr, 1)

        @block.scalar
        def _(act):
            for n in range(turns):
                for k in range(0, banks, 2):
                    act.wait_ge(s_tr, n * banks + k + 1)
                    nc.scalar.copy(m.keys[1 - held[n]][:, 512 * k:512 * (k + 1)], bank[k][:, :]).then_inc(s_act, 1)
    return m.sorted_in


def decode(m, ctx, final):
    nc, sb, sem, bank = m.nc, m.sb, m.sem, m.bank
    keys, spare = m.keys[final], m.keys[1 - final]
    seg = sb("seg", [P, ROW], F32, ctx)
    seg_i = sb("seg_i", [P, ROW], I32, ctx)
    pad_f = spare
    before = sb("before", [P, 1], F32, ctx)
    key_t = sb("key_t", [P, TILES], F32, ctx)
    s_chain = sem("s_dec_dve")
    s_seg = sem("s_seg")
    s_before = sem("s_before")
    s_start = sem("s_start")
    s_tr = sem("s_dec_tr")
    s_moved = sem("s_dec_moved")
    squares = ROW // P
    rows = TILES // squares

    def tile_view(tile, k):
        return tile[:, 0:TILES].rearrange("p (r j) -> p j r", j=squares)[:, 4 * k:4 * k + 4, :]

    with nc.Block() as block:
        @block.sync
        def _(sp):
            sp.wait_ge(s_seg, 1)
            sp.dma_start(before[1:P, :], seg[0:P - 1, ROW - 1:ROW]).then_inc(s_before, 16)

        @block.tensor
        def _(pe):
            for n in range(2):
                if n == 1:
                    pe.wait_ge(s_start, 1)
                for k in range(8):
                    if n == 1:
                        pe.wait_ge(s_moved, k + 1)
                    for i in range(4):
                        j = 4 * k + i
                        last = pe.transpose(bank[k][:, i * P:(i + 1) * P], (keys, seg)[n][:, j * P:(j + 1) * P],
                                            m.ident[:, :])
                    last.then_inc(s_tr, 1)

        @block.scalar
        def _(act):
            for n in range(2):
                for k in range(8):
                    act.wait_ge(s_tr, 8 * n + k + 1)
                    squares4 = bank[k][:, :].rearrange("p (j r) -> p j r", j=4)[:, :, 0:rows]
                    if n == 0:
                        nc.scalar.copy(tile_view(key_t, k), squares4).then_inc(s_moved, 1)
                    else:
                        nc.scalar.mul(tile_view(m.pen, k), squares4, -BIG).then_inc(s_moved, 1)

        @block.vector
        def _(dve):
            c = Chain(dve, s_chain)
            key = keys[:, :].bitcast(I32)
            c.link(dve.memset(before[:, :], -1.0))
            c.link(dve.tensor_single_scalar(seg_i[:, :], key, NODE_MASK, ALU.bitwise_and))
            c.link(dve.tensor_scalar(pad_f[:, :], seg_i[:, :], float(NODE_MASK), None, ALU.is_equal))
            c.link(dve.tensor_scalar(seg_i[:, :], key, NODE_BITS, NODE_MASK, ALU.logical_shift_right, ALU.bitwise_and))
            dve.scalar_tensor_tensor(seg[:, :], seg_i[:, :], 2.0, pad_f[:, :], ALU.mult, ALU.add).then_inc(s_seg, 1)
            dve.wait_ge(s_seg, 1)
            c.link(dve.tensor_tensor(pad_f[:, 1:ROW], seg[:, 1:ROW], seg[:, 0:ROW - 1], ALU.not_equal))
            dve.wait_ge(s_before, 16)
            c.link(dve.tensor_tensor(pad_f[:, 0:1], seg[:, 0:1], before[:, :], ALU.not_equal))
            dve.tensor_copy(seg[:, :], pad_f[:, :]).then_inc(s_start, 1)

            dve.wait_ge(s_moved, 8)
            key = key_t[:, :].bitcast(I32)
            pad_t, place = seg_i[:, 0:TILES], spare[:, 0:TILES].bitcast(I32)
            c.link(dve.tensor_single_scalar(pad_t, key, NODE_MASK, ALU.bitwise_and))
            c.link(dve.tensor_scalar(m.row_of[:, 0:TILES], pad_t, float(N - 1), None, ALU.min))
            c.link(dve.tensor_scalar(m.place[:, 0:TILES], pad_t, float(NODE_MASK), FAR, ALU.is_equal, ALU.mult))
            c.link(dve.tensor_scalar(place, key, NODE_BITS, P - 1, ALU.logical_shift_right, ALU.bitwise_and))
            c.link(dve.tensor_tensor(m.place[:, 0:TILES], m.place[:, 0:TILES], place, ALU.add))
            dve.memset(m.place[:, TILES:TILES + PAD], 0.0)
            c.link(dve.memset(m.row_of[:, TILES:TILES + PAD], 0))


def attention(m, ctx):
    nc, sb, sem, bank = m.nc, m.sb, m.sem, m.bank
    U = 8
    V = 4
    steps = CHUNK_GROUPS // U
    GW = GROUP_TILES * D
    PAIRS = GROUP_TILES * HEADS
    rows = [sb(f"rows{k}", [P, GROUP_TILES, D], F32, ctx) for k in range(U)]
    rows2 = [sb(f"rows_again{k}", [P, GROUP_TILES, D], F32, ctx) for k in range(V)]
    stage = [sb(f"stage{k}", [P, GROUP_TILES], I32, ctx) for k in range(U)]
    hot = [sb(f"hot{k}", [P, GROUP_TILES, P], BF16, ctx) for k in range(2)]
    hot_t = [sb(f"hot_t{k}", [P, GROUP_TILES * P], BF16, ctx) for k in range(2)]
    hot2 = [sb(f"hot_sum{k}", [P, GROUP_TILES, P], F32, ctx) for k in range(2)]
    z = sb("z", [P, GROUP_TILES, D], F32, ctx)
    leaky = sb("leaky", [P, GROUP_TILES, D], F32, ctx)
    weighed = sb("weighed", [P, GROUP_TILES, D], F32, ctx)
    terms = [sb(f"terms{k}", [P, PAIRS, ACCW], F32, ctx) for k in range(2)]
    scores = sb("scores", [P, CHUNK_TILES, HEADS], F32, ctx)
    weights = sb("weights", [P, CHUNK_TILES, HEADS], F32, ctx)
    score_s = sb("score_s", [P, SCAN], F32, ctx)
    pen_s = sb("pen_s", [P, SCAN + 1], BF16, ctx)
    top_f = sb("top_f", [P, SCAN], F32, ctx)
    top = sb("top", [P, SCAN], F32, ctx)
    edge_cols = sb("edge_cols", [P, 4], F32, ctx)
    pen_cols = top_f[:, :].bitcast(BF16)[:, 0:SCAN]
    init = sb("init", [P, 1], F32, ctx)
    edge_rows = sb("edge_rows", [1, 4, P], F32, ctx)
    least = sb("least", [1, P], F32, ctx)
    ahead = sb("ahead", [1, P + HEADS], F32, ctx)
    back = sb("back", [1, P + HEADS], F32, ctx)
    back_in = sb("back_in", [1, P], F32, ctx)
    link = sb("link", [1, P], F32, ctx)
    again = sb("again", [1, HEADS + 1], F32, ctx)
    again_all = sb("again_all", [P, HEADS + 1], F32, ctx)
    is_node = sb("is_node", [P, BLOCKS], F32, ctx)
    factor = sb("factor", [P, BLOCKS, HEADS], F32, ctx)

    s_staged = sem("s_staged")
    s_pool = sem("s_pool")
    s_gath = [sem(f"s_gath{k}") for k in range(U)]
    s_store = [sem(f"s_store{k}") for k in range(U)]
    s_load = [sem(f"s_load{k}") for k in range(V)]
    s_hot = sem("s_hot")
    s_hot_ps = sem("s_hot_ps")
    s_hot_t = sem("s_hot_t")
    s_left = sem("s_left")
    s_z, s_leaky, s_weighed = sem("s_z"), sem("s_leaky"), sem("s_weighed")
    s_score = sem("s_score")
    s_dve_wait = sem("s_dve_wait")
    s_terms = sem("s_terms")
    s_sum_ps = sem("s_sum_ps")
    s_acc = sem("s_acc")
    s_chain = sem("s_att_dve")
    s_sorted_scores, s_sorted_pens = sem("s_sorted_scores"), sem("s_sorted_pens")
    s_fill = sem("s_fill")
    s_score_s, s_pen_s = sem("s_score_s"), sem("s_pen_s")
    s_edge, s_edge_ps = sem("s_edge"), sem("s_edge_ps")
    s_arg, s_exp = sem("s_arg"), sem("s_exp")
    s_again_arg, s_again = sem("s_again_arg"), sem("s_again")
    s_back = sem("s_back")
    s_weights_act, s_weights_dve = sem("s_weights_act"), sem("s_weights_dve")

    fills = [(g, min(4, ROW_TILES - g)) for g in range(0, ROW_TILES, 4)]
    n_fills = len(fills)
    act_fills = (n_fills + 1) // 2
    edges_before = [0]
    for c in range(CHUNKS):
        edges_before.append(edges_before[-1] + (4 if c == 0 else 6))

    def loop(eng, c, body):
        body(c, 0)
        with eng.Fori(1, steps) as i:
            body(c, i)

    def score_group(c, i, k):
        return c * CHUNK_GROUPS + U * i + k

    def sum_group(c, i, k):
        return (c - 1) * CHUNK_GROUPS + U * i + k

    with nc.Block() as block:
        @block.gpsimd
        def _(pool):
            def body(c, i):
                for k in range(U):
                    use = c * steps + i
                    q = score_group(c, i, k)
                    at_least(pool, s_store[k], use * 16)
                    at_least(pool, s_z, q - U + 1)
                    pool.wait_ge(s_staged, q + 1)
                    pool.sem_inc(s_pool, 1)
                    for g in range(GROUP_TILES):
                        pool.indirect_dma_start(rows[k][:, g, :], None, m.gr_table[:, :],
                                                bass.IndirectOffsetOnAxis(stage[k][:, g:g + 1], 0)).then_inc(s_gath[k], 16)
            for c in range(CHUNKS):
                loop(pool, c, body)

        @block.sync
        def _(sp):
            def body(c, i):
                for k in range(U):
                    if c >= 1:
                        at_least(sp, s_terms, sum_group(c, i, k) - V + 1)
                        sp.dma_start(rows2[k % V][:, :, :].rearrange("p g f -> p (g f)"),
                                     m.gr_rows[bass.ds(sum_group(c, i, k), 1), :, :].rearrange("q p f -> p (q f)")
                                     ).then_inc(s_load[k % V], 16)
                    if c < CHUNKS:
                        sp.wait_ge(s_gath[k], (c * steps + i + 1) * 16 * GROUP_TILES)
                        sp.dma_start(m.gr_rows[bass.ds(score_group(c, i, k), 1), :, :].rearrange("q p f -> p (q f)"),
                                     rows[k][:, :, :].rearrange("p g f -> p (g f)")).then_inc(s_store[k], 16)
            for c in range(CHUNKS + 1):
                loop(sp, c, body)
                for k in range(U):
                    sp.wait_ge(s_store[k], min(c + 1, CHUNKS) * steps * 16)

        @block.tensor
        def _(pe):
            def body(c, i):
                for k in range(U):
                    q, r = score_group(c, i, k), sum_group(c, i, k)
                    if c < CHUNKS:
                        left(q + 1, (k + 1) % 2)
                    if c >= 1:
                        pe.wait_ge(s_terms, r + 1)
                        at_least(pe, s_acc, r - 1)
                        for g in range(GROUP_TILES):
                            last = pe.matmul(bank[4 + k % 2][:, 0:HEADS * ACCW], hot2[k % 2][:, g, :],
                                             terms[k % 2][:, g * HEADS:(g + 1) * HEADS, :].rearrange("p h w -> p (h w)"),
                                             start=g == 0, stop=g == GROUP_TILES - 1)
                        last.then_inc(s_sum_ps, 1)
                    if c < CHUNKS:
                        turn(q + 2, k % 2)

            def left(q, slot):
                blk = pe.value_load(m.blk_i[0:1, bass.ds(q, 1)], min_val=0, max_val=BLOCKS - 1)
                pe.wait_ge(s_hot_t, q + 1)
                at_least(pe, s_z, q - 1)
                for g in range(GROUP_TILES):
                    for part in range(3):
                        last = pe.matmul(bank[2 + slot][:, g * D:(g + 1) * D], hot_t[slot][:, g * P:(g + 1) * P],
                                         m.gl_parts[:, bass.ds(blk, 1), part * D:(part + 1) * D].rearrange("p b f -> p (b f)"),
                                         start=part == 0, stop=part == 2)
                last.then_inc(s_left, 1)

            def turn(q, slot):
                pe.wait_ge(s_hot, q + 1)
                at_least(pe, s_hot_t, q - 1)
                turned = bank[slot][:, :].bitcast(BF16)
                for g in range(GROUP_TILES):
                    last = pe.transpose(turned[:, g * P:(g + 1) * P], hot[slot][:, g, :], m.ident_bf[:, :])
                last.then_inc(s_hot_ps, 1)

            def scan(c):
                e = edges_before[c] + max(c - 1, 0)
                pe.wait_ge(s_sorted_scores, c + 1)
                pe.wait_ge(s_sorted_pens, c + 1)
                for j, (g0, n) in enumerate(fills):
                    if j:
                        pe.wait_ge(s_score_s, c * n_fills + j)
                        pe.wait_ge(s_pen_s, c * n_fills + j)
                    for g in range(n):
                        last = pe.transpose(bank[6][:, g * P:(g + 1) * P], top[:, (g0 + g) * P:(g0 + g + 1) * P],
                                            m.ident[:, :])
                    last.then_inc(s_fill, 1)
                    pens = bank[7][:, :].bitcast(BF16)
                    for g in range(n):
                        last = pe.transpose(pens[:, g * P:(g + 1) * P], pen_cols[:, (g0 + g) * P:(g0 + g + 1) * P],
                                            m.ident_bf[:, :])
                    last.then_inc(s_fill, 1)
                pe.wait_ge(s_score_s, (c + 1) * n_fills)
                pe.wait_ge(s_pen_s, (c + 1) * n_fills)
                pe.wait_ge(s_edge, e + 1)
                for v in range(3):
                    last = pe.transpose(bank[6][0:1, v * P:(v + 1) * P], edge_cols[:, v:v + 1], m.ident[:, :])
                last.then_inc(s_edge_ps, 1)
                pe.wait_ge(s_edge, e + 2)
                pe.transpose(bank[7][:, 0:1], ahead[0:1, 0:P], m.ident[0:1, 0:1]).then_inc(s_edge_ps, 1)
                pe.wait_ge(s_edge, e + 3)
                pe.transpose(bank[6][0:1, 0:P], edge_cols[:, 3:4], m.ident[:, :]).then_inc(s_edge_ps, 1)
                pe.wait_ge(s_edge, e + 4)
                pe.transpose(bank[7][:, 0:1], back_in[0:1, :], m.ident[0:1, 0:1]).then_inc(s_edge_ps, 1)
                if c:
                    pe.wait_ge(s_edge, e + 5)
                    pe.transpose(bank[6][0:1, 0:P], edge_cols[:, 3:4], m.ident[:, :]).then_inc(s_edge_ps, 1)
                    pe.wait_ge(s_edge, e + 6)
                    pe.wait_ge(s_again, c)
                    pe.matmul(bank[7][:, 0:HEADS + 1], m.ones[0:1, :], again[:, :], start=True, stop=True
                              ).then_inc(s_edge_ps, 1)
                    pe.wait_ge(s_edge, edges_before[c + 1] + c)
                pe.wait_ge(s_exp, c + 1)
                for j, (g0, n) in enumerate(fills):
                    if j >= 2:
                        if j % 2:
                            pe.wait_ge(s_weights_dve, c * (n_fills - act_fills) + j // 2)
                        else:
                            pe.wait_ge(s_weights_act, c * act_fills + j // 2)
                    for g in range(n):
                        last = pe.transpose(bank[6 + j % 2][:, g * P:(g + 1) * P],
                                            score_s[:, (g0 + g) * P:(g0 + g + 1) * P], m.ident[:, :])
                    last.then_inc(s_back, 1)

            turn(0, 0)
            turn(1, 1)
            left(0, 0)
            for c in range(CHUNKS + 1):
                loop(pe, c, body)
                if c < CHUNKS:
                    scan(c)

        def weights_by_tile(g0, n):
            return weights[:, :, :].rearrange("p (r g) h -> p g r h", g=ROW_TILES)[:, g0:g0 + n]

        @block.scalar
        def _(act):
            def move_hot(q, slot):
                at_least(act, s_left, q - 1)
                act.wait_ge(s_hot_ps, q + 1)
                nc.scalar.copy(hot_t[slot][:, :], bank[slot][:, :].bitcast(BF16)[:, 0:GROUP_TILES * P]
                               ).then_inc(s_hot_t, 1)

            def body(c, i):
                for k in range(U):
                    move_hot(score_group(c, i, k) + 2, k % 2)

            for q in range(2):
                move_hot(q, q)
            for c in range(CHUNKS):
                loop(act, c, body)
                act.wait_ge(s_score, (c + 1) * CHUNK_GROUPS)
                nc.scalar.copy(top[:, :].rearrange("p (g r h) -> p g r h", g=ROW_TILES, h=HEADS),
                               scores[:, :, :].rearrange("p (r g) h -> p g r h", g=ROW_TILES)
                               ).then_inc(s_sorted_scores, 1)
                for j, (g0, n) in enumerate(fills):
                    act.wait_ge(s_fill, 2 * (c * n_fills + j) + 1)
                    nc.scalar.copy(score_s[:, g0 * P:(g0 + n) * P], bank[6][:, 0:n * P]).then_inc(s_score_s, 1)
                if c:
                    act.wait_ge(s_again_arg, c)
                    nc.scalar.activation(again[:, 0:HEADS], again[:, 0:HEADS], ACT.Exp).then_inc(s_again, 1)
                act.wait_ge(s_arg, c + 1)
                nc.scalar.activation(score_s[:, :], score_s[:, :], ACT.Exp).then_inc(s_exp, 1)
                for j, (g0, n) in enumerate(fills):
                    if j % 2 == 0:
                        act.wait_ge(s_back, c * n_fills + j + 1)
                        nc.scalar.copy(weights_by_tile(g0, n),
                                       bank[6][:, 0:n * P].rearrange("p (g r h) -> p g r h", g=n, h=HEADS)
                                       ).then_inc(s_weights_act, 1)

        @block.vector
        def _(dve):
            chain = Chain(dve, s_chain)
            att = m.att[:, :].unsqueeze(1).to_broadcast([P, GROUP_TILES, D])
            places = m.iota_row[:, :].unsqueeze(1).to_broadcast([P, GROUP_TILES, P])

            def hot_of(out, q):
                at = m.place[:, bass.ds(q * GROUP_TILES, GROUP_TILES)].unsqueeze(2).to_broadcast([P, GROUP_TILES, P])
                return dve.tensor_tensor(out[:, :, :], places, at, ALU.is_equal)

            def stage_of(k, q):
                return dve.tensor_scalar(stage[k][:, :], m.row_of[:, bass.ds(q * GROUP_TILES, GROUP_TILES)], 0.0, None,
                                         ALU.add)

            def body(c, i):
                for k in range(U):
                    q, r = score_group(c, i, k), sum_group(c, i, k)
                    use = c * steps + i
                    if c < CHUNKS:
                        dve.wait_ge(s_left, q + 1)
                        dve.wait_ge(s_gath[k], (use + 1) * 16 * GROUP_TILES)
                        dve.tensor_tensor(z[:, :, :], bank[2 + k % 2][:, 0:GW].rearrange("p (g f) -> p g f", f=D),
                                          rows[k][:, :, :], ALU.add).then_inc(s_z, 1)
                    if c >= 1:
                        at_least(dve, s_sum_ps, r - 1)
                        hot_of(hot2[k % 2], r)
                    if c < CHUNKS:
                        dve.wait_ge(s_z, q + 1)
                        dve.scalar_tensor_tensor(leaky[:, :, :], z[:, :, :], SLOPE, z[:, :, :], ALU.mult,
                                                 ALU.max).then_inc(s_leaky, 1)
                    if c >= 1:
                        weight = weights[:, bass.ds((U * i + k) * GROUP_TILES, GROUP_TILES), :].rearrange("p g h -> p (g h)")
                        dve.wait_ge(s_load[k % V], ((use - steps) * (U // V) + k // V + 1) * 16)
                        dve.tensor_tensor(terms[k % 2][:, :, 0:DH],
                                          rows2[k % V][:, :, :].rearrange("p g (h f) -> p (g h) f", f=DH),
                                          weight.unsqueeze(2).to_broadcast([P, PAIRS, DH]), ALU.mult)
                        dve.tensor_copy(terms[k % 2][:, :, DH:ACCW], weight.unsqueeze(2)).then_inc(s_terms, 1)
                    if c < CHUNKS:
                        dve.wait_ge(s_leaky, q + 1)
                        dve.tensor_tensor(weighed[:, :, :], leaky[:, :, :], att, ALU.mult).then_inc(s_weighed, 1)
                        dve.wait_ge(s_hot_ps, q + 1)
                        hot_of(hot[k % 2], q + 2).then_inc(s_hot, 1)
                        at_least(dve, s_gath[(k - 1) % U], (use + (k > 0)) * 16 * GROUP_TILES)
                        stage_of((k - 1) % U, q + U - 1).then_inc(s_staged, 1)
                        dve.wait_ge(s_weighed, q + 1)
                        dve.sem_inc(s_dve_wait, 1)
                        nc_reduce(dve, scores[:, bass.ds((U * i + k) * GROUP_TILES, GROUP_TILES), :].rearrange("p g h -> p (g h)"),
                                  weighed[:, :, :].rearrange("p g (h f) -> p (g h) f", f=DH)).then_inc(s_score, 1)
                    if c >= 1 and not (isinstance(i, int) and i == 0 and k == 0):
                        accumulate(r - 1, (k - 1) % 2)

            def accumulate(r, slot):
                blk = dve.value_load(m.blk_i[0:1, bass.ds(r, 1)], min_val=0, max_val=BLOCKS - 1)
                sums = m.acc[:, bass.ds(blk, 1), :].rearrange("p b w -> p (b w)")
                at_least(dve, s_acc, r)
                dve.wait_ge(s_sum_ps, r + 1)
                dve.tensor_tensor(sums, sums, bank[4 + slot][:, 0:HEADS * ACCW], ALU.add).then_inc(s_acc, 1)

            def scan(c):
                pens = m.pen[:, c * CHUNK_TILES:(c + 1) * CHUNK_TILES].rearrange("p (r g) -> p g r", g=ROW_TILES)
                dve.tensor_copy(pen_cols.rearrange("p (g r h) -> p g r h", g=ROW_TILES, h=HEADS),
                                pens.unsqueeze(3).to_broadcast([P, ROW_TILES, CHUNK_ROWS, HEADS])
                                ).then_inc(s_sorted_pens, 1)
                for j, (g0, n) in enumerate(fills):
                    dve.wait_ge(s_fill, 2 * (c * n_fills + j) + 2)
                    dve.tensor_copy(pen_s[:, g0 * P:(g0 + n) * P], bank[7][:, :].bitcast(BF16)[:, 0:n * P]
                                    ).then_inc(s_pen_s, 1)
                dve.wait_ge(s_pen_s, (c + 1) * n_fills)
                dve.wait_ge(s_score_s, (c + 1) * n_fills)
                down = slice(None, None, -1)
                chain.link(dve.tensor_tensor_scan(top_f[:, :], pen_s[:, 0:SCAN], score_s[:, :], -BIG, ALU.add, ALU.max))
                dve.tensor_copy(edge_cols[:, 0:1], pen_s[:, 0:1])
                nc_reduce(dve, edge_cols[:, 1:2], pen_s[:, 1:SCAN], ALU.min)
                dve.tensor_copy(edge_cols[:, 2:3], top_f[:, SCAN - 1:SCAN]).then_inc(s_edge, 1)
                dve.wait_ge(s_edge_ps, edges_before[c] + 1)
                chain.link(dve.tensor_copy(edge_rows[:, 0:3, :].rearrange("p v q -> p (v q)"), bank[6][0:1, 0:3 * P]))
                chain.link(dve.tensor_tensor(least[:, :], edge_rows[:, 0, :], edge_rows[:, 1, :], ALU.min))
                for h in range(HEADS):
                    chain.link(dve.tensor_tensor_scan(ahead[:, HEADS + h::HEADS], least[:, h::HEADS],
                                                      edge_rows[:, 2, h::HEADS], ahead[:, h:h + 1], ALU.add, ALU.max))
                dve.engine_nop().then_inc(s_edge, 1)
                dve.wait_ge(s_edge_ps, edges_before[c] + 2)
                chain.link(dve.tensor_copy(init[:, :], bank[7][:, 0:1]))
                chain.link(dve.tensor_tensor_scan(top_f[:, :], pen_s[:, 0:SCAN], score_s[:, :], init[:, :], ALU.add, ALU.max))
                chain.link(dve.tensor_tensor_scan(top[:, down], pen_s[:, 1:SCAN + 1][:, down], top_f[:, down], -BIG,
                                                  ALU.add, ALU.max))
                dve.tensor_copy(edge_cols[:, 3:4], top[:, 0:1]).then_inc(s_edge, 1)
                dve.wait_ge(s_edge_ps, edges_before[c] + 3)
                chain.link(dve.tensor_copy(edge_rows[:, 3, :], bank[6][0:1, 0:P]))
                chain.link(dve.tensor_tensor(link[:, 0:P - HEADS], edge_rows[:, 0, HEADS:P], edge_rows[:, 1, 0:P - HEADS],
                                             ALU.add))
                for h in range(HEADS):
                    chain.link(dve.tensor_tensor_scan(back[:, h:P:HEADS][:, down], link[:, h::HEADS][:, down],
                                                      edge_rows[:, 3, h::HEADS][:, down], back[:, P + h:P + h + 1],
                                                      ALU.add, ALU.max))
                dve.tensor_tensor(back_in[:, 0:P - HEADS], back[:, HEADS:P], edge_rows[:, 0, HEADS:P], ALU.add
                                  ).then_inc(s_edge, 1)
                dve.wait_ge(s_edge_ps, edges_before[c] + 4)
                chain.link(dve.tensor_copy(init[:, :], bank[7][:, 0:1]))
                chain.link(dve.tensor_tensor_scan(top[:, down], pen_s[:, 1:SCAN + 1][:, down], top_f[:, down], init[:, :],
                                                  ALU.add, ALU.max))
                if c:
                    dve.tensor_copy(edge_cols[:, 3:4], top[:, 0:1]).then_inc(s_edge, 1)
                    dve.wait_ge(s_edge_ps, edges_before[c] + 5)
                    chain.link(dve.tensor_copy(edge_rows[:, 3, :], bank[6][0:1, 0:P]))
                    chain.link(dve.tensor_tensor(again[:, 0:HEADS], ahead[:, 0:HEADS], edge_rows[:, 3, 0:HEADS],
                                                 ALU.subtract))
                    chain.link(dve.tensor_scalar(link[:, 0:HEADS], edge_rows[:, 0, 0:HEADS], 0.0, None, ALU.is_equal))
                    dve.tensor_tensor(again[:, 0:HEADS], again[:, 0:HEADS], link[:, 0:HEADS], ALU.mult
                                      ).then_inc(s_again_arg, 1)
                dve.tensor_tensor(score_s[:, :], score_s[:, :], top[:, :], ALU.subtract).then_inc(s_arg, 1)
                if c:
                    first, tile = c * CHUNK_GROUPS, c * CHUNK_TILES
                    dve.scalar_tensor_tensor(again[:, HEADS:HEADS + 1], m.blk_f[:, first:first + 1], float(P),
                                             m.place[0:1, tile:tile + 1], ALU.mult, ALU.add).then_inc(s_edge, 1)
                    dve.wait_ge(s_edge_ps, edges_before[c] + 6)
                    chain.link(dve.tensor_copy(again_all[:, :], bank[7][:, 0:HEADS + 1]))
                    dve.engine_nop().then_inc(s_edge, 1)
                    chain.link(dve.tensor_scalar(is_node[:, :], m.iota_node[:, :], again_all[:, HEADS:HEADS + 1], None,
                                                 ALU.is_equal))
                    chain.link(dve.tensor_scalar(again_all[:, 0:HEADS], again_all[:, 0:HEADS], -1.0, None, ALU.add))
                    for h in range(HEADS):
                        chain.link(dve.tensor_scalar(factor[:, :, h], is_node[:, :], again_all[:, h:h + 1], 1.0, ALU.mult,
                                                     ALU.add))
                    by_head = m.acc[:, :, :].rearrange("p b (h w) -> p (b h) w", w=ACCW)
                    chain.link(dve.tensor_tensor(by_head, by_head, factor[:, :, :].rearrange("p b h -> p (b h)").unsqueeze(2)
                                                 .to_broadcast([P, BLOCKS * HEADS, ACCW]), ALU.mult))
                chain.link(dve.tensor_copy(ahead[:, 0:HEADS], ahead[:, P:P + HEADS]))
                for j, (g0, n) in enumerate(fills):
                    if j % 2:
                        dve.wait_ge(s_back, c * n_fills + j + 1)
                        dve.tensor_copy(weights_by_tile(g0, n),
                                        bank[7][:, 0:n * P].rearrange("p (g r h) -> p g r h", g=n, h=HEADS)
                                        ).then_inc(s_weights_dve, 1)
                dve.wait_ge(s_weights_dve, (c + 1) * (n_fills - act_fills))
                dve.wait_ge(s_weights_act, (c + 1) * act_fills)

            chain.link(dve.memset(m.acc[:, :, :], 0.0))
            dve.memset(pen_s[:, SCAN:SCAN + 1], 0.0)
            dve.memset(ahead[:, :], -BIG)
            dve.memset(back[:, :], -BIG)
            dve.memset(back_in[:, :], -BIG)
            chain.link(dve.memset(link[:, :], -BIG))
            for k in range(U - 1):
                stage_of(k, k).then_inc(s_staged, 1)
            for q in range(2):
                hot_of(hot[q], q).then_inc(s_hot, 1)
            for c in range(CHUNKS + 1):
                loop(dve, c, body)
                if c >= 1:
                    accumulate(c * CHUNK_GROUPS - 1, (U - 1) % 2)
                    dve.wait_ge(s_acc, c * CHUNK_GROUPS)
                if c < CHUNKS:
                    scan(c)


def attention_nodes(m, ctx):
    nc, sb, sem, bank = m.nc, m.sb, m.sem, m.bank
    share = sb("share", [P, BLOCKS * HEADS], F32, ctx)
    mixed = sb("mixed", [P, BLOCKS, D], F32, ctx)
    mixed_t = [sb(f"mixed_t{i}", [D, 512], F32, ctx) for i in range(2)]
    normed_t = [sb(f"normed_t{i}", [D, 512], F32, ctx) for i in range(2)]
    hidden_t = [sb(f"hidden_t{i}", [D, 512], F32, ctx) for i in range(2)]
    s_x = sem("s_x_again")
    s_chain = sem("s_nodes0_dve")
    s_mixed = sem("s_mixed")
    s_in_ps, s_in = sem("s_in_ps"), sem("s_in")
    s_hid_ps, s_hid = sem("s_hid_ps"), sem("s_hid")
    s_out_ps, s_add = sem("s_out_ps"), sem("s_add")
    s_var, s_std = sem("s_var1"), sem("s_std1")
    s_h2, s_stored = sem("s_h2"), sem("s_h2_stored")
    rounds = [(b, min(4, BLOCKS - b)) for b in range(0, BLOCKS, 4)]

    with nc.Block() as block:
        @block.sync
        def _(sp):
            sp.wait_ge(s_mixed, 2)
            load_blocks(sp, m.x, m.t["x"], s_x)
            sp.wait_ge(s_h2, 1)
            store_blocks(sp, m.h2_table, m.h, s_stored)
            sp.wait_ge(s_stored, 32)

        @block.tensor
        def _(pe):
            pe.wait_ge(s_mixed, 1)
            for r, (b, n) in enumerate(rounds):
                if r:
                    pe.wait_ge(s_in, 2 * r)
                for i in range(n):
                    pe.transpose(bank[0][0:D, i * P:(i + 1) * P], mixed[:, b + i, :], m.ident[:, :])
                    last = pe.transpose(bank[1][0:D, i * P:(i + 1) * P], m.h[:, b + i, :], m.ident[:, :])
                last.then_inc(s_in_ps, 1)
                pe.wait_ge(s_in, 2 * r + 2)
                if r >= 2:
                    pe.wait_ge(s_hid, r - 1)
                hid = bank[2 + r % 2][0:D, 0:n * P]
                pe.matmul(hid, m.w1t_out[:, :], mixed_t[r % 2][:, 0:n * P], start=True, stop=False)
                pe.matmul(hid, m.w1t_h[:, :], normed_t[r % 2][:, 0:n * P], start=False, stop=True).then_inc(s_hid_ps, 1)
                pe.wait_ge(s_hid, r + 1)
                if r >= 2:
                    pe.wait_ge(s_add, r - 1)
                for i in range(n):
                    last = pe.matmul(bank[4 + r % 2][:, i * D:(i + 1) * D], hidden_t[r % 2][:, i * P:(i + 1) * P],
                                     m.w2t[:, :], start=True, stop=True)
                last.then_inc(s_out_ps, 1)

        @block.scalar
        def _(act):
            for r, (b, n) in enumerate(rounds):
                act.wait_ge(s_in_ps, r + 1)
                nc.scalar.copy(mixed_t[r % 2][:, 0:n * P], bank[0][0:D, 0:n * P]).then_inc(s_in, 1)
                nc.scalar.copy(normed_t[r % 2][:, 0:n * P], bank[1][0:D, 0:n * P]).then_inc(s_in, 1)
                act.wait_ge(s_hid_ps, r + 1)
                if r >= 2:
                    act.wait_ge(s_out_ps, r - 1)
                nc.scalar.activation(hidden_t[r % 2][:, 0:n * P], bank[2 + r % 2][0:D, 0:n * P], ACT.Gelu,
                                     bias=m.b1_l0[:, :]).then_inc(s_hid, 1)
            act.wait_ge(s_var, 1)
            nc.scalar.activation(m.rstd[:, :], m.var[:, :], ACT.Sqrt).then_inc(s_std, 1)

        @block.vector
        def _(dve):
            chain = Chain(dve, s_chain)
            by_head = m.acc[:, :, :].rearrange("p b (h w) -> p (b h) w", w=ACCW)
            chain.link(dve.tensor_scalar(share[:, :].unsqueeze(2), by_head[:, :, DH:ACCW], 1e-16, None, ALU.add))
            chain.link(dve.reciprocal(share[:, :], share[:, :]))
            dve.tensor_tensor(mixed[:, :, :].rearrange("p b (h f) -> p (b h) f", f=DH), by_head[:, :, 0:DH],
                              share[:, :].unsqueeze(2).to_broadcast([P, BLOCKS * HEADS, DH]), ALU.mult
                              ).then_inc(s_mixed, 1)
            chain.link(dve.memset(m.x[:, BLOCKS - 1, :], 0.0))
            dve.engine_nop().then_inc(s_mixed, 1)
            dve.wait_ge(s_x, 32)
            chain.link(dve.tensor_tensor(m.x[:, :, :], m.x[:, :, :],
                                         m.b2_l0[:, :].unsqueeze(1).to_broadcast([P, BLOCKS, D]), ALU.add))
            for r, (b, n) in enumerate(rounds):
                dve.wait_ge(s_out_ps, r + 1)
                dve.tensor_tensor(m.x[:, b:b + n, :], m.x[:, b:b + n, :],
                                  bank[4 + r % 2][:, 0:n * D].rearrange("p (b f) -> p b f", f=D), ALU.add
                                  ).then_inc(s_add, 1)
            dve.wait_ge(s_add, len(rounds))
            layernorm_steps(m, chain, dve, m.x, m.h, mixed, s_var, s_std, 1).then_inc(s_h2, 1)


def messages(m, ctx):
    nc, sb, sem, bank = m.nc, m.sb, m.sem, m.bank
    attrs = m.t["edge_attr_64"]
    rows = [sb(f"message{k}", [P, EDGE_TILES, D], F32, ctx) for k in range(2)]
    edge = [sb(f"edge{k}", [P, EDGE_TILES, D], F32, ctx) for k in range(2)]
    stage = [sb(f"edge_stage{k}", [P, EDGE_TILES], I32, ctx) for k in range(2)]
    hot = sb("edge_hot", [P, EDGE_TILES, P], F32, ctx)
    nodes = sb("nodes", [P, BLOCKS * P], F32, ctx)
    dst_f = sb("dst_f", [P, EDGE_COLS], F32, ctx)
    minus = sb("minus", [P, EDGE_COLS], F32, ctx)
    span = sb("span", [P, 2, EDGE_GROUPS], F32, ctx)
    spans = sb("spans", [P, 2, EDGE_GROUPS], F32, ctx)
    span_i = sb("span_i", [1, 2, EDGE_GROUPS], I32, ctx)
    blocks_f = sb("blocks_f", [1, 2, EDGE_GROUPS], F32, ctx)
    step_f = sb("step_f", [1, EDGE_GROUPS + 1], F32, ctx)
    step_of = sb("step_of", [1, EDGE_GROUPS + 1], I32, ctx)
    shift = sb("shift", [1, EDGE_GROUPS], I32, ctx)
    s_nodes = sem("s_nodes")
    s_span, s_spans = sem("s_span"), sem("s_spans")
    s_tables = sem("s_tables")
    s_chain = sem("s_msg_dve")
    s_staged, s_pool = sem("s_edge_staged"), sem("s_edge_pool")
    s_gath = [sem(f"s_message{k}") for k in range(2)]
    s_edge = [sem(f"s_edge{k}") for k in range(2)]
    s_message = sem("s_message")
    s_hot = sem("s_edge_hot")
    s_sum_ps = sem("s_edge_sum_ps")
    s_agg = sem("s_agg")
    s_done = sem("s_done")
    last_i = EDGE_GROUPS // 2 - 1

    def loop(eng, body):
        body(0)
        with eng.Fori(1, last_i) as i:
            body(i)
        body(last_i)

    def steps_of(eng, g):
        first = eng.value_load(step_of[0:1, bass.ds(g, 1)], min_val=0, max_val=BLOCKS * EDGE_GROUPS)
        end = eng.value_load(step_of[0:1, bass.ds(g + 1, 1)], min_val=0, max_val=BLOCKS * EDGE_GROUPS)
        return eng.Fori(first, end)

    with nc.Block() as block:
        @block.gpsimd
        def _(pool):
            pool.iota(nodes[:, :], [[1, BLOCKS * P]], base=0, channel_multiplier=0,
                      allow_small_or_imprecise_dtypes=True).then_inc(s_nodes, 1)
            pool.wait_ge(s_span, 1)
            pool.partition_all_reduce(spans[:, :, :].rearrange("p a g -> p (a g)"),
                                      span[:, :, :].rearrange("p a g -> p (a g)"), P,
                                      bass.bass_isa.ReduceOp.max).then_inc(s_spans, 1)

            def body(i):
                for k in range(2):
                    g = 2 * i + k
                    at_least(pool, s_done, g - 1)
                    pool.wait_ge(s_staged, g + 1)
                    pool.sem_inc(s_pool, 1)
                    for e in range(EDGE_TILES):
                        pool.indirect_dma_start(rows[k][:, e, :], None, m.h2_table[:, :],
                                                bass.IndirectOffsetOnAxis(stage[k][:, e:e + 1], 0)).then_inc(s_gath[k], 16)
            loop(pool, body)

        @block.sync
        def _(sp):
            full = attrs[0:FULL_EDGES, :].rearrange("(g p t) f -> g p (t f)", p=P, t=EDGE_TILES)
            tail = attrs[FULL_EDGES:E, :].rearrange("(p t) f -> p (t f)", t=EDGE_TILES)

            def body(i):
                for k in range(2):
                    g = 2 * i + k
                    at_least(sp, s_message, g - 1)
                    if isinstance(g, int) and g == EDGE_GROUPS - 1:
                        sp.dma_start(edge[k][0:TAIL_PARTS, :, :].rearrange("p t f -> p (t f)"), tail).then_inc(s_edge[k], 16)
                    else:
                        sp.dma_start(edge[k][:, :, :].rearrange("p t f -> p (t f)"),
                                     full[bass.ds(g, 1), :, :].rearrange("g p f -> p (g f)")).then_inc(s_edge[k], 16)
            loop(sp, body)

        @block.tensor
        def _(pe):
            pe.wait_ge(s_tables, 1)

            def body(i):
                for k in range(2):
                    with steps_of(pe, 2 * i + k) as r:
                        pe.wait_ge(s_hot, r + 1)
                        for e in range(EDGE_TILES):
                            last = pe.matmul(bank[0][:, 0:D], hot[:, e, :], rows[k][:, e, :], start=e == 0,
                                             stop=e == EDGE_TILES - 1)
                        last.then_inc(s_sum_ps, 1)
            loop(pe, body)

        @block.vector
        def _(dve):
            c = Chain(dve, s_chain)

            def stage_of(k, g):
                return dve.tensor_scalar(stage[k][:, :], m.src[:, bass.ds(g * EDGE_TILES, EDGE_TILES)], 0.0, None, ALU.add)

            stage_of(0, 0).then_inc(s_staged, 1)
            dve.memset(m.agg[:, :, :], 0.0).then_inc(s_agg, 1)
            c.link(dve.memset(minus[:, FULL_COLS:EDGE_COLS], -float(P * BLOCKS)))
            c.link(dve.tensor_copy(dst_f[:, :], m.dst[:, :]))
            dve.tensor_scalar(minus[:, 0:FULL_COLS], dst_f[:, 0:FULL_COLS], -1.0, None, ALU.mult)
            c.link(dve.tensor_scalar(minus[0:TAIL_PARTS, FULL_COLS:EDGE_COLS],
                                     dst_f[0:TAIL_PARTS, FULL_COLS:EDGE_COLS], -1.0, None, ALU.mult))
            for v, tile in enumerate((dst_f, minus)):
                c.link(nc_reduce(dve, span[:, v, :], tile[:, :].rearrange("p (g t) -> p g t", t=EDGE_TILES), ALU.max))
            dve.engine_nop().then_inc(s_span, 1)
            dve.wait_ge(s_spans, 1)
            c.link(dve.tensor_copy(span_i[:, 0, :], spans[0:1, 0, :]))
            c.link(dve.tensor_scalar(span_i[:, 1, :], spans[0:1, 1, :], -1.0, None, ALU.mult))
            c.link(dve.tensor_single_scalar(span_i[:, :, :], span_i[:, :, :], LOG_P, ALU.logical_shift_right))
            c.link(dve.tensor_copy(blocks_f[:, :, :], span_i[:, :, :]))
            c.link(dve.scalar_tensor_tensor(blocks_f[:, 0, :], blocks_f[:, 0, :], 1.0, blocks_f[:, 1, :], ALU.add,
                                            ALU.subtract))
            c.link(dve.memset(step_f[:, :], 1.0))
            c.link(dve.tensor_tensor_scan(step_f[:, 1:EDGE_GROUPS + 1], step_f[:, 1:EDGE_GROUPS + 1], blocks_f[:, 0, :], 0.0,
                                          ALU.mult, ALU.add))
            c.link(dve.memset(step_f[:, 0:1], 0.0))
            c.link(dve.tensor_copy(step_of[:, :], step_f[:, :]))
            c.link(dve.scalar_tensor_tensor(shift[:, :], blocks_f[:, 1, :], float(SHIFT), step_f[:, 0:EDGE_GROUPS], ALU.add,
                                            ALU.subtract))
            dve.engine_nop().then_inc(s_tables, 1)
            dve.wait_ge(s_nodes, 1)

            def body(i):
                for k in range(2):
                    g = 2 * i + k
                    if not (isinstance(g, int) and g == EDGE_GROUPS - 1):
                        at_least(dve, s_gath[1 - k], (i + k) * 16 * EDGE_TILES)
                        stage_of(1 - k, g + 1).then_inc(s_staged, 1)
                    dve.wait_ge(s_edge[k], (i + 1) * 16)
                    dve.wait_ge(s_gath[k], (i + 1) * 16 * EDGE_TILES)
                    dve.tensor_tensor(rows[k][:, :, :], rows[k][:, :, :], edge[k][:, :, :], ALU.add).then_inc(s_message, 1)
                    moved = dve.value_load(shift[0:1, bass.ds(g, 1)], min_val=SHIFT - BLOCKS * EDGE_GROUPS,
                                           max_val=SHIFT + BLOCKS)
                    with steps_of(dve, g) as r:
                        blk = nc.s_assert_within(r + moved - SHIFT, 0, BLOCKS - 1, skip_runtime_bounds_check_because=
                                                 "the steps of a group are the blocks of its dst")
                        to = dst_f[:, bass.ds(g * EDGE_TILES, EDGE_TILES)].unsqueeze(2).to_broadcast([P, EDGE_TILES, P])
                        dve.tensor_tensor(hot[:, :, :], nodes[:, bass.ds(blk * P, P)].unsqueeze(1).to_broadcast(
                            [P, EDGE_TILES, P]), to, ALU.is_equal).then_inc(s_hot, 1)
                        dve.wait_ge(s_agg, r + 1)
                        dve.wait_ge(s_sum_ps, r + 1)
                        sums = m.agg[:, bass.ds(blk, 1), :].rearrange("p b f -> p (b f)")
                        dve.tensor_tensor(sums, sums, bank[0][:, 0:D], ALU.add).then_inc(s_agg, 1)
                    dve.engine_nop().then_inc(s_done, 1)
            loop(dve, body)


def message_nodes(m, ctx):
    nc, sb, sem, bank = m.nc, m.sb, m.sem, m.bank
    agg_t = [sb(f"agg_t{i}", [D, 512], F32, ctx) for i in range(2)]
    hidden_t = [sb(f"wide_t{i}", [2 * D, 512], F32, ctx) for i in range(2)]
    y = sb("y", [D, BLOCKS * P], F32, ctx)
    square = sb("y_square", [D, N], F32, ctx)
    parts = 50
    part = sb("part_sums", [D, parts], F32, ctx)
    stats = sb("stats", [D, 4], F32, ctx)
    s_chain = sem("s_nodes1_dve")
    s_in_ps, s_in = sem("s_agg_ps"), sem("s_agg_t")
    s_hid_ps, s_hid = sem("s_wide_ps"), sem("s_wide")
    s_y_ps, s_y = sem("s_y_ps"), sem("s_y")
    s_var, s_std = sem("s_var2"), sem("s_std2")
    s_norm = sem("s_norm")
    s_back, s_add = sem("s_y_back"), sem("s_result")
    s_out = sem("s_out")
    rounds = [(b, min(4, BLOCKS - b)) for b in range(0, BLOCKS, 4)]
    turns = [(b, min(8, BLOCKS - b)) for b in range(0, BLOCKS, 8)]

    with nc.Block() as block:
        @block.tensor
        def _(pe):
            for r, (b, n) in enumerate(rounds):
                if r >= 2:
                    pe.wait_ge(s_in, r - 1)
                for i in range(n):
                    last = pe.transpose(bank[r % 2][0:D, i * P:(i + 1) * P], m.agg[:, b + i, :], m.ident[:, :])
                last.then_inc(s_in_ps, 1)
                pe.wait_ge(s_in, r + 1)
                if r >= 2:
                    pe.wait_ge(s_hid, r - 1)
                pe.matmul(bank[2 + r % 2][:, 0:n * P], m.w1_l1[:, :], agg_t[r % 2][:, 0:n * P], start=True, stop=True
                          ).then_inc(s_hid_ps, 1)
                pe.wait_ge(s_hid, r + 1)
                if r >= 2:
                    pe.wait_ge(s_y, r - 1)
                pe.matmul(bank[4 + r % 2][0:D, 0:n * P], m.w2_l1[:, :], hidden_t[r % 2][:, 0:n * P], start=True,
                          stop=True).then_inc(s_y_ps, 1)
            pe.wait_ge(s_norm, 1)
            for r, (b, n) in enumerate(turns):
                if r >= 2:
                    pe.wait_ge(s_add, r - 1)
                for i in range(n):
                    last = pe.transpose(bank[6 + r % 2][:, i * D:(i + 1) * D], y[:, (b + i) * P:(b + i + 1) * P],
                                        m.ident[0:D, 0:D])
                last.then_inc(s_back, 1)

        @block.scalar
        def _(act):
            for r, (b, n) in enumerate(rounds):
                act.wait_ge(s_in_ps, r + 1)
                nc.scalar.copy(agg_t[r % 2][:, 0:n * P], bank[r % 2][0:D, 0:n * P]).then_inc(s_in, 1)
                act.wait_ge(s_hid_ps, r + 1)
                nc.scalar.activation(hidden_t[r % 2][:, 0:n * P], bank[2 + r % 2][:, 0:n * P], ACT.Relu,
                                     bias=m.b1_l1[:, :]).then_inc(s_hid, 1)
                act.wait_ge(s_y_ps, r + 1)
                nc.scalar.activation(y[:, b * P:(b + n) * P], bank[4 + r % 2][0:D, 0:n * P], ACT.Identity,
                                     bias=m.cols_l1[:, 0:1]).then_inc(s_y, 1)
            act.wait_ge(s_var, 1)
            nc.scalar.activation(stats[:, 2:3], stats[:, 1:2], ACT.Sqrt).then_inc(s_std, 1)

        @block.vector
        def _(dve):
            c = Chain(dve, s_chain)
            dve.wait_ge(s_y, len(rounds))
            c.link(nc_reduce(dve, part[:, :], y[:, 0:N].rearrange("p (a n) -> p a n", a=parts)))
            c.link(nc_reduce(dve, stats[:, 0:1], part[:, :]))
            c.link(dve.tensor_scalar(stats[:, 0:1], stats[:, 0:1], 1.0 / N, None, ALU.mult))
            c.link(dve.tensor_scalar(y[:, :], y[:, :], stats[:, 0:1], None, ALU.subtract))
            c.link(dve.tensor_tensor(square[:, :], y[:, 0:N], y[:, 0:N], ALU.mult))
            c.link(nc_reduce(dve, part[:, :], square[:, :].rearrange("p (a n) -> p a n", a=parts)))
            c.link(nc_reduce(dve, stats[:, 1:2], part[:, :]))
            dve.tensor_scalar(stats[:, 1:2], stats[:, 1:2], 1.0 / N, BN_EPS, ALU.mult, ALU.add).then_inc(s_var, 1)
            dve.wait_ge(s_std, 1)
            c.link(dve.reciprocal(stats[:, 2:3], stats[:, 2:3]))
            c.link(dve.tensor_tensor(stats[:, 3:4], stats[:, 2:3], stats[:, 2:3], ALU.mult))
            c.link(dve.tensor_tensor(stats[:, 3:4], stats[:, 3:4], stats[:, 1:2], ALU.mult))
            c.link(dve.tensor_scalar(stats[:, 3:4], stats[:, 3:4], -0.5, 1.5, ALU.mult, ALU.add))
            c.link(dve.tensor_tensor(stats[:, 2:3], stats[:, 2:3], stats[:, 3:4], ALU.mult))
            c.link(dve.tensor_tensor(stats[:, 2:3], stats[:, 2:3], m.cols_l1[:, 1:2], ALU.mult))
            dve.tensor_scalar(y[:, :], y[:, :], stats[:, 2:3], m.cols_l1[:, 2:3], ALU.mult, ALU.add).then_inc(s_norm, 1)
            for r, (b, n) in enumerate(turns):
                dve.wait_ge(s_back, r + 1)
                dve.tensor_tensor(m.x[:, b:b + n, :], m.x[:, b:b + n, :],
                                  bank[6 + r % 2][:, 0:n * D].rearrange("p (b f) -> p b f", f=D), ALU.add
                                  ).then_inc(s_add, 1)

        @block.sync
        def _(sp):
            sp.wait_ge(s_add, len(turns))
            store_blocks(sp, m.out, m.x, s_out)
            sp.wait_ge(s_out, 32)


_INS = ['x', 'src', 'dst', 'edge_attr_64', 'L0_gnn_Wl', 'L0_gnn_Wr', 'L0_gnn_att', 'L0_gnn_W1', 'L0_gnn_b1',
        'L0_gnn_W2', 'L0_gnn_b2', 'L1_gnn_W1', 'L1_gnn_b1', 'L1_gnn_W2', 'L1_gnn_b2', 'L1_gnn_bn_gamma',
        'L1_gnn_bn_beta']


def kernel(**inputs):
    import concourse.bacc as bacc
    from concourse.bass_utils import run_bass_kernel_spmd

    nc = bacc.Bacc("TRN2", target_bir_lowering=False, num_devices=1)
    arrays, t = {}, {}
    for name in _INS:
        a = np.ascontiguousarray(inputs[name])
        arrays[f"in_{name}"] = a
        t[name] = nc.dram_tensor(f"in_{name}", a.shape, mybir.dt.from_np(a.dtype), kind="ExternalInput").ap()
    out = nc.dram_tensor("out_0", (N, D), F32, kind="ExternalOutput").ap()
    build(nc, t, out)
    r = run_bass_kernel_spmd(nc, [arrays], core_ids=[0])
    return r.results[0]["out_0"]
```

```python
from contextlib import ExitStack

import numpy as np

import concourse.bass as bass
from concourse import mybir

F32 = mybir.dt.float32
BF16 = mybir.dt.bfloat16
I32 = mybir.dt.int32
ALU = mybir.AluOpType
ACT = mybir.ActivationFunctionType
AX = mybir.AxisListType

P = 128
N, E, D = 6250, 200000, 64
HEADS = 4
DH = D // HEADS
SLOPE = 0.2
LN_EPS = 1e-5
BN_EPS = 1e-5
BLOCKS = -(-N // P)
LAST = N - (BLOCKS - 1) * P

EDGE_TILES = 8
EDGE_GROUP = EDGE_TILES * P
EDGE_GROUPS = -(-E // EDGE_GROUP)
FULL_EDGES = (EDGE_GROUPS - 1) * EDGE_GROUP
TAIL_PARTS = (E - FULL_EDGES) // EDGE_TILES
EDGE_COLS = EDGE_GROUPS * EDGE_TILES
FULL_COLS = EDGE_COLS - EDGE_TILES

GROUP_TILES = 4
GROUP = GROUP_TILES * P
LOG_P, LOG_ROW = 7, 12
ROW = 1 << LOG_ROW
SORT_LOG = LOG_P + LOG_ROW
NODE_BITS = 13
NODE_MASK = (1 << NODE_BITS) - 1
KEY_BIT = 1 << (2 * NODE_BITS + 1)
NO_KEY = float(np.array([KEY_BIT | ((1 << 2 * NODE_BITS) - 1)], np.int32).view(np.float32)[0])
CHUNKS = 13
CHUNK_ROWS = 32
GROUPS = 832
assert GROUPS * GROUP >= 2 * E + BLOCKS * (GROUP - 1) and GROUPS * GROUP <= 1 << SORT_LOG
TILES = GROUPS * GROUP_TILES
CHUNK_GROUPS = GROUPS // CHUNKS
CHUNK_TILES = TILES // CHUNKS
ROW_TILES = CHUNK_TILES // CHUNK_ROWS
SCAN = ROW_TILES * P
GATHER_SLOTS = 16
PAD = GATHER_SLOTS * GROUP_TILES
FAR = 8192.0
BIG = 1e30
ACCW = DH + 1
SHIFT = 16384


def at_least(eng, sem, value):
    if isinstance(value, int) and value <= 0:
        return
    eng.wait_ge(sem, value)


def load_blocks(eng, tile, dram, sem):
    full = (BLOCKS - 1) * P
    eng.dma_start(tile[:, 0:BLOCKS - 1, :], dram[0:full, :].rearrange("(b p) f -> p b f", p=P)).then_inc(sem, 16)
    eng.dma_start(tile[0:LAST, BLOCKS - 1, :], dram[full:N, :]).then_inc(sem, 16)


def store_blocks(eng, dram, tile, sem):
    full = (BLOCKS - 1) * P
    eng.dma_start(dram[0:full, :].rearrange("(b p) f -> p b f", p=P), tile[:, 0:BLOCKS - 1, :]).then_inc(sem, 16)
    eng.dma_start(dram[full:N, :], tile[0:LAST, BLOCKS - 1, :]).then_inc(sem, 16)


class Chain:

    def __init__(self, eng, sem):
        self.eng, self.sem, self.n, self.turns = eng, sem, 0, 0

    def link(self, ins):
        self.n += 1
        ins.then_inc(self.sem, 1)
        self.eng.wait_ge(self.sem, self.turns + self.n)


class Memory:
    pass


def layernorm_steps(m, chain, dve, x, h, square, s_var, s_std, turn):
    chain.link(nc_reduce(dve, m.mean[:, :], x[:, :, :]))
    chain.link(dve.tensor_scalar(m.mean[:, :], m.mean[:, :], 1.0 / D, None, ALU.mult))
    spread = m.mean[:, :].unsqueeze(2).to_broadcast([P, BLOCKS, D])
    chain.link(dve.tensor_tensor(h[:, :, :], x[:, :, :], spread, ALU.subtract))
    chain.link(dve.tensor_tensor(square[:, :, :], h[:, :, :], h[:, :, :], ALU.mult))
    chain.link(nc_reduce(dve, m.var[:, :], square[:, :, :]))
    dve.tensor_scalar(m.var[:, :], m.var[:, :], 1.0 / D, LN_EPS, ALU.mult, ALU.add).then_inc(s_var, 1)
    dve.wait_ge(s_std, turn)
    chain.link(dve.reciprocal(m.rstd[:, :], m.rstd[:, :]))
    chain.link(dve.tensor_tensor(m.mean[:, :], m.rstd[:, :], m.rstd[:, :], ALU.mult))
    chain.link(dve.tensor_tensor(m.mean[:, :], m.mean[:, :], m.var[:, :], ALU.mult))
    chain.link(dve.tensor_scalar(m.mean[:, :], m.mean[:, :], -0.5, 1.5, ALU.mult, ALU.add))
    chain.link(dve.tensor_tensor(m.rstd[:, :], m.rstd[:, :], m.mean[:, :], ALU.mult))
    spread = m.rstd[:, :].unsqueeze(2).to_broadcast([P, BLOCKS, D])
    return dve.scalar_tensor_tensor(h[:, :, :], h[:, :, :], 0.0, spread, ALU.max, ALU.mult)


def nc_reduce(dve, out, in_, op=ALU.add):
    return dve.tensor_reduce(out, in_, AX.X, op)


def build(nc, t, out, stop=None):
    with ExitStack() as whole:
        m = Memory()
        m.nc, m.t, m.out = nc, t, out

        def sb(name, shape, dt, ctx=whole):
            return ctx.enter_context(nc.sbuf_tensor(name, shape, dt))

        def sem(name):
            return whole.enter_context(nc.semaphore(name))

        m.sb, m.sem = sb, sem
        m.bank = [whole.enter_context(nc.psum_tensor(f"bank{i}", [P, 512], F32)) for i in range(8)]

        m.gr_table = nc.dram_tensor("gr_table", (N, D), F32).ap()
        m.h2_table = nc.dram_tensor("h2_table", (N, D), F32).ap()
        m.gr_rows = nc.dram_tensor("gr_rows", (GROUPS, P, GROUP_TILES * D), F32).ap()

        m.h = sb("h_sb", [P, BLOCKS, D], F32)
        m.src = sb("src_sb", [P, EDGE_COLS], I32)
        m.dst = sb("dst_sb", [P, EDGE_COLS], I32)
        m.ident = sb("ident", [P, P], F32)
        m.ident_bf = sb("ident_bf", [P, P], BF16)
        m.ones = sb("ones", [P, P], F32)
        m.iota_row = sb("iota_row", [P, P], F32)
        m.iota_node = sb("iota_node", [P, BLOCKS], F32)
        m.att = sb("att_sb", [P, D], F32)
        m.w1t_out = sb("w1t_out", [D, D], F32)
        m.w1t_h = sb("w1t_h", [D, D], F32)
        m.b1_l0 = sb("b1_l0", [D, 1], F32)
        m.w2t = sb("w2t", [D, D], F32)
        m.b2_l0 = sb("b2_l0", [P, D], F32)
        m.w1_l1 = sb("w1_l1", [D, 2 * D], F32)
        m.b1_l1 = sb("b1_l1", [2 * D, 1], F32)
        m.w2_l1 = sb("w2_l1", [2 * D, D], F32)
        m.cols_l1 = sb("cols_l1", [D, 3], F32)
        m.mean = sb("mean", [P, BLOCKS], F32)
        m.var = sb("var", [P, BLOCKS], F32)
        m.rstd = sb("rstd", [P, BLOCKS], F32)
        m.blk_i = sb("blk_i", [1, GROUPS + 2], I32)
        m.blk_f = sb("blk_f", [1, GROUPS], F32)
        m.step_of = sb("step_of", [1, EDGE_GROUPS + 1], I32)
        m.first_of = sb("first_of", [1, EDGE_GROUPS], I32)
        m.shift = sb("shift", [1, EDGE_GROUPS], I32)

        m.acc = sb("acc", [P, BLOCKS, HEADS * ACCW], F32)
        layer0, keys_ctx = (whole.enter_context(ExitStack()) for _ in range(2))
        m.gl_parts = sb("gl_parts", [P, BLOCKS, 3 * D], BF16, layer0)
        m.place = sb("place", [P, TILES + PAD], F32, layer0)
        m.row_of = sb("row_of", [P, TILES + PAD], I32, layer0)
        m.pen = sb("pen", [P, TILES], BF16, layer0)

        m.keys = [sb("keys0", [P, ROW], F32, keys_ctx), sb("keys1", [P, ROW], F32, keys_ctx)]
        with ExitStack() as ctx:
            prepare(m, ctx)
        if stop == "prepare":
            return m
        with ExitStack() as ctx:
            final = sort(m, ctx)
        if stop == "sort":
            return m
        with ExitStack() as ctx:
            decode(m, ctx, final)
        keys_ctx.close()
        if stop == "decode":
            return m
        with ExitStack() as ctx:
            attention(m, ctx)
        layer0.close()
        if stop == "attention":
            return m
        m.x = sb("x_sb", [P, BLOCKS, D], F32)
        m.agg = sb("agg", [P, BLOCKS, D], F32)
        m.nodes = sb("nodes", [P, BLOCKS * P], F32)
        m.dst_f = sb("dst_f", [P, EDGE_COLS], F32)
        with ExitStack() as ctx:
            attention_nodes(m, ctx)
        if stop == "nodes0":
            return m
        with ExitStack() as ctx:
            messages(m, ctx)
        with ExitStack() as ctx:
            message_nodes(m, ctx)
        return m


def prepare(m, ctx):
    nc, t, sb, sem, bank = m.nc, m.t, m.sb, m.sem, m.bank
    m.x = sb("x_in", [P, BLOCKS, D], F32, ctx)
    w_l0 = sb("w_l0", [D, 2, D], F32, ctx)
    w1_l0 = sb("w1_l0", [D, 2 * D], F32, ctx)
    w2_l0 = sb("w2_l0", [D, D], F32, ctx)
    w_lr_t = sb("w_lr_t", [D, 2 * D], F32, ctx)
    ht = [sb(f"ht{i}", [D, 4 * P], F32, ctx) for i in range(2)]
    gl = sb("gl", [P, BLOCKS, D], F32, ctx)
    gr = sb("gr", [P, BLOCKS, D], F32, ctx)
    src_f = sb("src_f", [P, 2 * EDGE_COLS], F32, ctx)
    below = sb("below", [P, BLOCKS], F32, ctx)
    counts = sb("counts", [P, BLOCKS], F32, ctx)
    room = sb("room", [P, BLOCKS], I32, ctx)
    room_f = sb("room_f", [P, BLOCKS], F32, ctx)
    ends = sb("ends", [P, BLOCKS], F32, ctx)
    end_col = sb("end_col", [BLOCKS, 1], F32, ctx)
    span = sb("span", [P, 2, EDGE_GROUPS], F32, ctx)
    spans = sb("spans", [P, 2, EDGE_GROUPS], F32, ctx)
    span_i = sb("span_i", [1, 2, EDGE_GROUPS], I32, ctx)
    blocks_f = sb("blocks_f", [1, 2, EDGE_GROUPS], F32, ctx)
    step_f = sb("step_f", [1, EDGE_GROUPS + 1], F32, ctx)
    bias = sb("bias", [P, BLOCKS], F32, ctx)
    iota_group = sb("iota_group", [BLOCKS, GROUPS], F32, ctx)
    past = sb("past", [BLOCKS, GROUPS], F32, ctx)
    ordinal = sb("ordinal", [P, GROUP_TILES], F32, ctx)
    pad_key = sb("pad_key", [P, BLOCKS], I32, ctx)
    unused = sb("unused", [P, BLOCKS, GROUP_TILES], I32, ctx)
    junk, junk_act = (m.keys[1][:, i * ROW // 2:(i + 1) * ROW // 2].bitcast(BF16)[:, 0:2 * EDGE_COLS] for i in range(2))

    s_init = sem("s_init")
    s_edges = sem("s_edges")
    s_x = sem("s_x")
    s_weights = sem("s_weights")
    s_const = sem("s_const")
    s_ident = sem("s_ident")
    s_var0, s_std0 = sem("s_var0"), sem("s_std0")
    s_h = sem("s_h")
    s_wt_ps, s_wt = sem("s_wt_ps"), sem("s_wt")
    s_ht_ps, s_ht = sem("s_ht_ps"), sem("s_ht")
    s_lr_ps = sem("s_lr_ps")
    s_lr = sem("s_lr")
    s_grt = sem("s_grt")
    s_cnt, s_cnt_ps = sem("s_cnt"), sem("s_cnt_ps")
    s_end, s_end_ps = sem("s_end"), sem("s_end_ps")
    s_past, s_past_ps = sem("s_past"), sem("s_past_ps")
    s_src_f, s_cnt_act = sem("s_src_f"), sem("s_cnt_act")
    s_span, s_spans = sem("s_span"), sem("s_spans")
    s_chain = sem("s_prep_dve")

    rounds = [(b, min(4, BLOCKS - b)) for b in range(0, BLOCKS, 4)]
    VECTOR_COUNTS = 28

    with nc.Block() as block:
        @block.sync
        def _(sp):
            sp.wait_ge(s_init, 1)
            load_blocks(sp, m.x, t["x"], s_x)
            sp.wait_ge(s_init, 2)
            for dram, tile in ((t["src"], m.src), (t["dst"], m.dst)):
                sp.dma_start(tile[:, 0:FULL_COLS].rearrange("p (g t) -> p g t", t=EDGE_TILES),
                             dram[0:FULL_EDGES].rearrange("(g p t) -> p g t", p=P, t=EDGE_TILES)).then_inc(s_edges, 16)
                sp.dma_start(tile[0:TAIL_PARTS, FULL_COLS:EDGE_COLS],
                             dram[FULL_EDGES:E].rearrange("(p t) -> p t", t=EDGE_TILES)).then_inc(s_edges, 16)
            sp.wait_ge(s_lr, len(rounds))
            store_blocks(sp, m.gr_table, gr, s_grt)
            sp.wait_ge(s_grt, 32)

        @block.scalar
        def _(act):
            for dram, tile in (
                (t["L0_gnn_Wl"], w_l0[:, 0, :]), (t["L0_gnn_Wr"], w_l0[:, 1, :]),
                (t["L0_gnn_W1"], w1_l0[:, :]), (t["L0_gnn_W2"], w2_l0[:, :]),
                (t["L0_gnn_att"].rearrange("a h d -> a (h d)").to_broadcast([P, D]), m.att[:, :]),
                (t["L0_gnn_b1"].unsqueeze(1), m.b1_l0[:, :]),
                (t["L0_gnn_b2"].unsqueeze(0).to_broadcast([P, D]), m.b2_l0[:, :]),
                (t["L1_gnn_W1"], m.w1_l1[:, :]), (t["L1_gnn_b1"].unsqueeze(1), m.b1_l1[:, :]),
                (t["L1_gnn_W2"], m.w2_l1[:, :]),
                (t["L1_gnn_b2"].unsqueeze(1), m.cols_l1[:, 0:1]),
                (t["L1_gnn_bn_gamma"].unsqueeze(1), m.cols_l1[:, 1:2]),
                (t["L1_gnn_bn_beta"].unsqueeze(1), m.cols_l1[:, 2:3]),
            ):
                act.dma_start(tile, dram).then_inc(s_weights, 16)
            act.wait_ge(s_var0, 1)
            nc.scalar.activation(m.rstd[:, :], m.var[:, :], ACT.Sqrt).then_inc(s_std0, 1)
            for r, (b, n) in enumerate(rounds):
                act.wait_ge(s_ht_ps, r + 1)
                if r >= 2:
                    act.wait_ge(s_lr_ps, r - 1)
                nc.scalar.copy(ht[r % 2][:, 0:n * P], bank[r % 2][0:D, 0:n * P]).then_inc(s_ht, 1)
                act.wait_ge(s_lr_ps, r + 1)
                terms = bank[2 + r % 2][:, 0:n * P].rearrange("p (b w f) -> p b w f", w=2, f=D)
                nc.scalar.copy(gl[:, b:b + n, :], terms[:, :, 0, :])
                nc.scalar.copy(gr[:, b:b + n, :], terms[:, :, 1, :]).then_inc(s_lr, 1)
            act.wait_ge(s_src_f, 1)
            for b in range(VECTOR_COUNTS, BLOCKS):
                at_least(act, s_cnt_act, b - VECTOR_COUNTS)
                nc.scalar.activation(junk_act, src_f[:, :], ACT.Sign, bias=bias[:, b:b + 1],
                                     accum_out=below[:, b:b + 1]).then_inc(s_cnt_act, 1)

        @block.gpsimd
        def _(pool):
            pool.memset(m.ident[:, :], 0.0).then_inc(s_ident, 1)
            pool.iota(m.iota_row[:, :], [[1, P]], base=0, channel_multiplier=0,
                      allow_small_or_imprecise_dtypes=True).then_inc(s_const, 1)
            pool.iota(m.iota_node[:, :], [[P, BLOCKS]], base=0, channel_multiplier=1,
                      allow_small_or_imprecise_dtypes=True).then_inc(s_const, 1)
            pool.iota(iota_group[:, :], [[1, GROUPS]], base=0, channel_multiplier=0,
                      allow_small_or_imprecise_dtypes=True).then_inc(s_const, 1)
            pool.iota(ordinal[:, :], [[P, GROUP_TILES]], base=0, channel_multiplier=1,
                      allow_small_or_imprecise_dtypes=True).then_inc(s_const, 1)
            pool.iota(pad_key[:, :], [[1, BLOCKS]], base=0, channel_multiplier=0).then_inc(s_const, 1)
            pool.wait_ge(s_ident, 1)
            pool.affine_select(out=m.ident[:, :], in_=m.ident[:, :], compare_op=ALU.not_equal, fill=1.0, base=0,
                               pattern=[[-1, P]], channel_multiplier=1).then_inc(s_ident, 1)
            pool.wait_ge(s_ident, 2)
            pool.tensor_copy(m.ident_bf[:, :], m.ident[:, :]).then_inc(s_const, 1)
            pool.wait_ge(s_span, 1)
            pool.partition_all_reduce(spans[:, :, :].rearrange("p a g -> p (a g)"),
                                      span[:, :, :].rearrange("p a g -> p (a g)"), P,
                                      bass.bass_isa.ReduceOp.max).then_inc(s_spans, 1)

        @block.tensor
        def _(pe):
            pe.wait_ge(s_weights, 16 * 13)
            pe.wait_ge(s_ident, 2)
            pieces = (w_l0[:, 0, :], w_l0[:, 1, :], w1_l0[:, 0:D], w1_l0[:, D:2 * D], w2_l0[:, :])
            for i, w in enumerate(pieces):
                last = pe.transpose(bank[4][0:D, i * D:(i + 1) * D], w, m.ident[0:D, 0:D])
            last.then_inc(s_wt_ps, 1)
            pe.wait_ge(s_h, 1)
            pe.wait_ge(s_wt, 1)
            for r, (b, n) in enumerate(rounds):
                if r >= 2:
                    pe.wait_ge(s_ht, r - 1)
                for i in range(n):
                    last = pe.transpose(bank[r % 2][0:D, i * P:(i + 1) * P], m.h[:, b + i, :], m.ident[:, :])
                last.then_inc(s_ht_ps, 1)
                pe.wait_ge(s_ht, r + 1)
                if r >= 2:
                    pe.wait_ge(s_lr, r - 1)
                for i in range(n):
                    last = pe.matmul(bank[2 + r % 2][:, i * P:(i + 1) * P], ht[r % 2][:, i * P:(i + 1) * P],
                                     w_lr_t[:, :], start=True, stop=True)
                last.then_inc(s_lr_ps, 1)
            pe.wait_ge(s_cnt, 1)
            pe.matmul(bank[5][:, 0:BLOCKS], m.ones[:, :], below[:, :], start=True, stop=True).then_inc(s_cnt_ps, 1)
            pe.wait_ge(s_end, 1)
            pe.transpose(bank[6][0:BLOCKS, 0:P], ends[:, :], m.ident[:, :]).then_inc(s_end_ps, 1)
            pe.wait_ge(s_past, 1)
            half = GROUPS // 2
            for i in range(2):
                last = pe.matmul(bank[6 + i][:, 0:half], m.ones[0:BLOCKS, :], past[:, i * half:(i + 1) * half],
                                 start=True, stop=True)
            last.then_inc(s_past_ps, 1)

        @block.vector
        def _(dve):
            c = Chain(dve, s_chain)
            dve.memset(m.x[:, BLOCKS - 1, :], 0.0).then_inc(s_init, 1)
            dve.memset(m.src[:, FULL_COLS:EDGE_COLS], 0)
            dve.memset(m.dst[:, FULL_COLS:EDGE_COLS], -1).then_inc(s_init, 1)
            dve.memset(src_f[:, :], FAR)
            dve.memset(m.keys[0][:, :], NO_KEY)
            c.link(dve.memset(m.ones[:, :], 1.0))
            dve.wait_ge(s_x, 32)
            layernorm_steps(m, c, dve, m.x, m.h, gl, s_var0, s_std0, 1).then_inc(s_h, 1)
            dve.wait_ge(s_wt_ps, 1)
            dve.tensor_copy(w_lr_t[:, :], bank[4][0:D, 0:2 * D])
            dve.tensor_copy(m.w1t_out[:, :], bank[4][0:D, 2 * D:3 * D])
            dve.tensor_copy(m.w1t_h[:, :], bank[4][0:D, 3 * D:4 * D])
            dve.tensor_copy(m.w2t[:, :], bank[4][0:D, 4 * D:5 * D]).then_inc(s_wt, 1)

            dve.wait_ge(s_edges, 64)
            ends_of = (m.src, m.dst)
            for way in range(2):
                a, b = ends_of[way], ends_of[1 - way]
                base = way * EDGE_COLS
                for parts, lo, hi in ((P, 0, FULL_COLS), (TAIL_PARTS, FULL_COLS, EDGE_COLS)):
                    key = m.keys[0][0:parts, base + lo:base + hi].bitcast(I32)
                    c.link(dve.scalar_tensor_tensor(key, a[0:parts, lo:hi], NODE_BITS, b[0:parts, lo:hi],
                                                    ALU.logical_shift_left, ALU.bitwise_or))
                    c.link(dve.tensor_single_scalar(key, key, KEY_BIT, ALU.bitwise_or))
                    c.link(dve.tensor_copy(src_f[0:parts, base + lo:base + hi], a[0:parts, lo:hi]))
            dve.wait_ge(s_const, 6)
            c.link(dve.tensor_scalar(bias[:, :], m.iota_node[:, :], m.iota_node[:, 0:1], -1.0, ALU.subtract, ALU.mult))
            c.link(dve.tensor_scalar(bias[:, :], bias[:, :], 0.5 - P, None, ALU.add))
            dve.engine_nop().then_inc(s_src_f, 1)
            nc_reduce(dve, span[:, 0, :], m.dst[:, :].rearrange("p (g t) -> p g t", t=EDGE_TILES), ALU.max)
            c.link(nc_reduce(dve, span[:, 1, :], src_f[:, EDGE_COLS:].rearrange("p (g t) -> p g t", t=EDGE_TILES), ALU.min))
            dve.tensor_scalar(span[:, 1, :], span[:, 1, :], -1.0, None, ALU.mult).then_inc(s_span, 1)
            for b in range(VECTOR_COUNTS):
                c.link(dve.tensor_scalar(junk, src_f[:, :], float(P * (b + 1)), None, ALU.is_lt, ALU.add,
                                         accum_out=below[:, b:b + 1]))
            dve.wait_ge(s_cnt_act, BLOCKS - VECTOR_COUNTS)
            c.link(dve.tensor_scalar(below[:, VECTOR_COUNTS:], below[:, VECTOR_COUNTS:], -0.5, float(EDGE_COLS), ALU.mult,
                                     ALU.add))
            dve.engine_nop().then_inc(s_cnt, 1)
            dve.wait_ge(s_lr, len(rounds))
            for part in range(3):
                piece = m.gl_parts[:, :, part * D:(part + 1) * D]
                c.link(dve.tensor_copy(piece, gl[:, :, :]))
                if part < 2:
                    c.link(dve.tensor_tensor(gl[:, :, :], gl[:, :, :], piece, ALU.subtract))

            dve.wait_ge(s_spans, 1)
            c.link(dve.tensor_copy(span_i[:, 0, :], spans[0:1, 0, :]))
            c.link(dve.tensor_scalar(span_i[:, 1, :], spans[0:1, 1, :], -1.0, None, ALU.mult))
            c.link(dve.tensor_single_scalar(span_i[:, :, :], span_i[:, :, :], LOG_P, ALU.logical_shift_right))
            c.link(dve.tensor_copy(blocks_f[:, :, :], span_i[:, :, :]))
            c.link(dve.tensor_copy(m.first_of[:, :], blocks_f[:, 1, :]))
            c.link(dve.tensor_tensor(blocks_f[:, 0, :], blocks_f[:, 0, :], blocks_f[:, 1, :], ALU.subtract))
            c.link(dve.memset(step_f[:, :], 1.0))
            c.link(dve.tensor_tensor_scan(step_f[:, 1:EDGE_GROUPS + 1], step_f[:, 1:EDGE_GROUPS + 1], blocks_f[:, 0, :], 0.0,
                                          ALU.mult, ALU.add))
            c.link(dve.memset(step_f[:, 0:1], 0.0))
            c.link(dve.tensor_copy(m.step_of[:, :], step_f[:, :]))
            c.link(dve.scalar_tensor_tensor(m.shift[:, :], blocks_f[:, 1, :], float(SHIFT + 1), step_f[:, 0:EDGE_GROUPS],
                                            ALU.add, ALU.subtract))

            dve.wait_ge(s_cnt_ps, 1)
            c.link(dve.tensor_copy(counts[:, :], bank[5][:, 0:BLOCKS]))
            c.link(dve.tensor_copy(below[:, :], counts[:, :]))
            c.link(dve.tensor_tensor(counts[:, 1:BLOCKS], below[:, 1:BLOCKS], below[:, 0:BLOCKS - 1], ALU.subtract))
            c.link(dve.tensor_scalar(room[:, :], counts[:, :], -1.0, float(1 << SORT_LOG), ALU.mult, ALU.add))
            c.link(dve.tensor_single_scalar(room[:, :], room[:, :], GROUP - 1, ALU.bitwise_and))
            c.link(dve.tensor_copy(room_f[:, :], room[:, :]))
            c.link(dve.tensor_tensor(counts[:, :], counts[:, :], room_f[:, :], ALU.add))
            c.link(dve.tensor_scalar(counts[:, :], counts[:, :], 1.0 / GROUP, None, ALU.mult))
            dve.tensor_tensor_scan(ends[:, :], m.ones[:, 0:BLOCKS], counts[:, :], 0.0, ALU.mult,
                                   ALU.add).then_inc(s_end, 1)
            dve.wait_ge(s_const, 6)
            c.link(dve.tensor_scalar(pad_key[:, :], pad_key[:, :], LOG_P + NODE_BITS,
                                     KEY_BIT | ((1 << LOG_P + NODE_BITS) - 1), ALU.logical_shift_left, ALU.bitwise_or))
            c.link(dve.tensor_tensor(unused[:, :, :], ordinal[:, :].unsqueeze(1).to_broadcast([P, BLOCKS, GROUP_TILES]),
                                     room_f[:, :].unsqueeze(2).to_broadcast([P, BLOCKS, GROUP_TILES]), ALU.is_ge))
            c.link(dve.tensor_scalar(unused[:, :, :], unused[:, :, :], 31, 31, ALU.logical_shift_left,
                                     ALU.arith_shift_right))
            c.link(dve.tensor_single_scalar(unused[:, :, :], unused[:, :, :], (1 << 2 * NODE_BITS) - 1, ALU.bitwise_and))
            pads = m.keys[0][:, 2 * EDGE_COLS:2 * EDGE_COLS + BLOCKS * GROUP_TILES].bitcast(I32)
            c.link(dve.tensor_tensor(pads.rearrange("p (b i) -> p b i", i=GROUP_TILES), unused[:, :, :],
                                     pad_key[:, :].unsqueeze(2).to_broadcast([P, BLOCKS, GROUP_TILES]), ALU.bitwise_or))
            dve.wait_ge(s_end_ps, 1)
            c.link(dve.tensor_copy(end_col[:, :], bank[6][0:BLOCKS, 0:1]))
            dve.tensor_scalar(past[:, :], iota_group[:, :], end_col[:, 0:1], None, ALU.is_ge).then_inc(s_past, 1)
            dve.wait_ge(s_past_ps, 1)
            half = GROUPS // 2
            for i in range(2):
                c.link(dve.tensor_scalar(m.blk_f[:, i * half:(i + 1) * half], bank[6 + i][0:1, 0:half],
                                         float(BLOCKS - 1), None, ALU.min))
            dve.memset(m.blk_i[:, GROUPS:], 0)
            c.link(dve.tensor_copy(m.blk_i[:, 0:GROUPS], m.blk_f[:, :]))


def sort(m, ctx):
    nc, sb, sem, bank = m.nc, m.sb, m.sem, m.bank
    bits = sb("bits", [P, LOG_P], I32, ctx)
    sign = sb("sign", [P, LOG_P + 1], F32, ctx)
    turn = sb("turn", [P, LOG_P + 1], F32, ctx)
    s_num = sem("s_num")
    s_chain = sem("s_sort_dve")
    s_ready = sem("s_sort_ready")
    s_tr = sem("s_sort_tr")
    s_moved = sem("s_sort_moved")
    turns = 2 * LOG_P
    HALF = ROW // 2
    banks = HALF // 512
    split = 3

    held = []

    with nc.Block() as block:
        @block.gpsimd
        def _(pool):
            pool.iota(bits[:, :], [[0, LOG_P]], base=0, channel_multiplier=1).then_inc(s_num, 1)

        @block.vector
        def _(dve):
            c = Chain(dve, s_chain)
            at = 0

            def one_pass(distance, at, lo=0, n=ROW):
                va, vb = (m.keys[i][:, lo:lo + n].rearrange("p (a two c) -> p two a c", two=2, c=distance)
                          for i in (at, 1 - at))
                dve.tensor_tensor(vb[:, 0], va[:, 0], va[:, 1], ALU.min)
                c.link(dve.tensor_tensor(vb[:, 1], va[:, 0], va[:, 1], ALU.max))

            def one_pass_by_runs(distance, at, run):
                form = "p (a way b two c) -> p way two a b c"
                sizes = dict(way=2, two=2, b=run // (2 * distance), c=distance)
                va, vb = (m.keys[i][:, :].rearrange(form, **sizes) for i in (at, 1 - at))
                for way, (low, high) in enumerate(((ALU.min, ALU.max), (ALU.max, ALU.min))):
                    dve.tensor_tensor(vb[:, way, 0], va[:, way, 0], va[:, way, 1], low)
                    last = dve.tensor_tensor(vb[:, way, 1], va[:, way, 0], va[:, way, 1], high)
                c.link(last)

            def passes(distances, at, lo, n):
                for i, distance in enumerate(distances):
                    one_pass(distance, (at + i) % 2, lo, n)

            dve.wait_ge(s_num, 1)
            for i in range(LOG_P):
                c.link(dve.tensor_scalar(bits[:, i:i + 1], bits[:, i:i + 1], i, 1, ALU.logical_shift_right,
                                         ALU.bitwise_and))
            c.link(dve.memset(sign[:, LOG_P:LOG_P + 1], 1.0))
            c.link(dve.tensor_scalar(sign[:, 0:LOG_P], bits[:, :], -2.0, 1.0, ALU.mult, ALU.add))
            c.link(dve.tensor_copy(turn[:, 0:1], sign[:, 0:1]))
            c.link(dve.tensor_tensor(turn[:, 1:LOG_P + 1], sign[:, 1:LOG_P + 1], sign[:, 0:LOG_P], ALU.mult))

            for stage in range(1, LOG_ROW):
                for i in reversed(range(stage)):
                    one_pass_by_runs(1 << i, at, 1 << stage)
                    at = 1 - at
            c.link(dve.tensor_scalar(m.keys[at][:, :], m.keys[at][:, :], turn[:, 0:1], None, ALU.mult))
            within = [1 << i for i in reversed(range(LOG_ROW))]
            for stage in range(LOG_ROW, SORT_LOG + 1):
                which = stage - LOG_ROW
                if stage > LOG_ROW:
                    across = [1 << i for i in reversed(range(which))]
                    for half in range(2):
                        dve.wait_ge(s_moved, ((len(held) - 1) * 2 + half + 1) * banks)
                        passes(across, at, half * HALF, HALF)
                        dve.engine_nop().then_inc(s_ready, 1)
                    at = (at + which) % 2
                    held.append(at)
                    at = 1 - at
                    for k in range(banks):
                        dve.wait_ge(s_moved, (len(held) * 2 - 1) * banks + k + 1)
                        va, vb = (m.keys[i][:, :].rearrange("p (two c) -> p two c", two=2)[:, :, 512 * k:512 * (k + 1)]
                                  for i in (at, 1 - at))
                        dve.tensor_tensor(vb[:, 0], va[:, 0], va[:, 1], ALU.min)
                        last = dve.tensor_tensor(vb[:, 1], va[:, 0], va[:, 1], ALU.max)
                    c.link(last)
                else:
                    one_pass(within[0], at)
                at = 1 - at
                if stage == SORT_LOG:
                    passes(within[1:], at, 0, ROW)
                    at = (at + LOG_ROW - 1) % 2
                else:
                    passes(within[1:-split], at, 0, ROW)
                    at = (at + LOG_ROW - 1 - split) % 2
                    for half in range(2):
                        passes(within[-split:], at, half * HALF, HALF)
                        done = m.keys[(at + split) % 2][:, half * HALF:(half + 1) * HALF]
                        c.link(dve.tensor_scalar(done, done, turn[:, which + 1:which + 2], None, ALU.mult))
                        dve.engine_nop().then_inc(s_ready, 1)
                    at = (at + split) % 2
                    held.append(at)
                    at = 1 - at
            m.sorted_in = at

        @block.tensor
        def _(pe):
            for n in range(turns):
                for half in range(2):
                    pe.wait_ge(s_ready, 2 * n + half + 1)
                    for k in range(half * banks, (half + 1) * banks):
                        for i in range(4):
                            j = 4 * k + i
                            last = pe.transpose(bank[k][:, i * P:(i + 1) * P], m.keys[held[n]][:, j * P:(j + 1) * P],
                                                m.ident[:, :])
                        last.then_inc(s_tr, 1)

        @block.scalar
        def _(act):
            for n in range(turns):
                for k in range(2 * banks):
                    act.wait_ge(s_tr, n * 2 * banks + k + 1)
                    nc.scalar.copy(m.keys[1 - held[n]][:, 512 * k:512 * (k + 1)], bank[k][:, :]).then_inc(s_moved, 1)
    return m.sorted_in


def decode(m, ctx, final):
    nc, sb, sem, bank = m.nc, m.sb, m.sem, m.bank
    keys, spare = m.keys[final], m.keys[1 - final]
    seg = sb("seg", [P, ROW], F32, ctx)
    seg_i = sb("seg_i", [P, ROW], I32, ctx)
    pad_f = spare
    before = sb("before", [P, 1], F32, ctx)
    key_t = sb("key_t", [P, TILES], F32, ctx)
    s_chain = sem("s_dec_dve")
    s_seg = sem("s_seg")
    s_before = sem("s_before")
    s_start = sem("s_start")
    s_tr = sem("s_dec_tr")
    s_moved = sem("s_dec_moved")
    squares = ROW // P
    rows = TILES // squares

    def tile_view(tile, k):
        return tile[:, 0:TILES].rearrange("p (r j) -> p j r", j=squares)[:, 4 * k:4 * k + 4, :]

    with nc.Block() as block:
        @block.sync
        def _(sp):
            sp.wait_ge(s_seg, 1)
            sp.dma_start(before[1:P, :], seg[0:P - 1, ROW - 1:ROW]).then_inc(s_before, 16)

        @block.tensor
        def _(pe):
            for n in range(2):
                if n == 1:
                    pe.wait_ge(s_start, 1)
                for k in range(8):
                    if n == 1:
                        pe.wait_ge(s_moved, k + 1)
                    for i in range(4):
                        j = 4 * k + i
                        last = pe.transpose(bank[k][:, i * P:(i + 1) * P], (keys, seg)[n][:, j * P:(j + 1) * P],
                                            m.ident[:, :])
                    last.then_inc(s_tr, 1)

        @block.scalar
        def _(act):
            for n in range(2):
                for k in range(8):
                    act.wait_ge(s_tr, 8 * n + k + 1)
                    squares4 = bank[k][:, :].rearrange("p (j r) -> p j r", j=4)[:, :, 0:rows]
                    if n == 0:
                        nc.scalar.copy(tile_view(key_t, k), squares4).then_inc(s_moved, 1)
                    else:
                        nc.scalar.mul(tile_view(m.pen, k), squares4, -BIG).then_inc(s_moved, 1)

        @block.vector
        def _(dve):
            c = Chain(dve, s_chain)
            key = keys[:, :].bitcast(I32)
            c.link(dve.memset(before[:, :], -1.0))
            c.link(dve.tensor_single_scalar(seg_i[:, :], key, NODE_MASK, ALU.bitwise_and))
            c.link(dve.tensor_scalar(pad_f[:, :], seg_i[:, :], float(NODE_MASK), None, ALU.is_equal))
            c.link(dve.tensor_scalar(seg_i[:, :], key, NODE_BITS, NODE_MASK, ALU.logical_shift_right, ALU.bitwise_and))
            dve.scalar_tensor_tensor(seg[:, :], seg_i[:, :], 2.0, pad_f[:, :], ALU.mult, ALU.add).then_inc(s_seg, 1)
            dve.wait_ge(s_seg, 1)
            c.link(dve.tensor_tensor(pad_f[:, 1:ROW], seg[:, 1:ROW], seg[:, 0:ROW - 1], ALU.not_equal))
            dve.wait_ge(s_before, 16)
            c.link(dve.tensor_tensor(pad_f[:, 0:1], seg[:, 0:1], before[:, :], ALU.not_equal))
            dve.tensor_copy(seg[:, :], pad_f[:, :]).then_inc(s_start, 1)

            dve.wait_ge(s_moved, 8)
            key = key_t[:, :].bitcast(I32)
            pad_t, place = seg_i[:, 0:TILES], spare[:, 0:TILES].bitcast(I32)
            c.link(dve.tensor_single_scalar(pad_t, key, NODE_MASK, ALU.bitwise_and))
            c.link(dve.tensor_scalar(m.row_of[:, 0:TILES], pad_t, float(N - 1), None, ALU.min))
            c.link(dve.tensor_scalar(m.place[:, 0:TILES], pad_t, float(NODE_MASK), FAR, ALU.is_equal, ALU.mult))
            c.link(dve.tensor_scalar(place, key, NODE_BITS, P - 1, ALU.logical_shift_right, ALU.bitwise_and))
            c.link(dve.tensor_tensor(m.place[:, 0:TILES], m.place[:, 0:TILES], place, ALU.add))
            dve.memset(m.place[:, TILES:TILES + PAD], 0.0)
            c.link(dve.memset(m.row_of[:, TILES:TILES + PAD], 0))


def attention(m, ctx):
    nc, sb, sem, bank = m.nc, m.sb, m.sem, m.bank
    U = GATHER_SLOTS
    V = 4
    steps = CHUNK_GROUPS // U
    GW = GROUP_TILES * D
    PAIRS = GROUP_TILES * HEADS
    rows = [sb(f"rows{k}", [P, GROUP_TILES, D], F32, ctx) for k in range(U)]
    rows2 = [sb(f"rows_again{k}", [P, GROUP_TILES, D], F32, ctx) for k in range(V)]
    stage = [sb(f"stage{k}", [P, GROUP_TILES], I32, ctx) for k in range(U)]
    hot = [sb(f"hot{k}", [P, GROUP_TILES, P], BF16, ctx) for k in range(2)]
    hot_t = [sb(f"hot_t{k}", [P, GROUP_TILES * P], BF16, ctx) for k in range(2)]
    hot2 = [sb(f"hot_sum{k}", [P, GROUP_TILES, P], F32, ctx) for k in range(2)]
    z = sb("z", [P, GROUP_TILES, D], F32, ctx)
    leaky = sb("leaky", [P, GROUP_TILES, D], F32, ctx)
    weighed = sb("weighed", [P, GROUP_TILES, D], F32, ctx)
    terms = [sb(f"terms{k}", [P, PAIRS, ACCW], F32, ctx) for k in range(2)]
    scores = sb("scores", [P, CHUNK_TILES, HEADS], F32, ctx)
    weights = sb("weights", [P, CHUNK_TILES, HEADS], F32, ctx)
    score_s = sb("score_s", [P, SCAN], F32, ctx)
    pen_s = sb("pen_s", [P, SCAN + 1], BF16, ctx)
    top_f = sb("top_f", [P, SCAN], F32, ctx)
    top = sb("top", [P, SCAN], F32, ctx)
    edge_cols = sb("edge_cols", [P, 4], F32, ctx)
    pen_cols = top_f[:, :].bitcast(BF16)[:, 0:SCAN]
    init = sb("init", [P, 1], F32, ctx)
    edge_rows = sb("edge_rows", [1, 4, P], F32, ctx)
    least = sb("least", [1, P], F32, ctx)
    ahead = sb("ahead", [1, P + HEADS], F32, ctx)
    back = sb("back", [1, P + HEADS], F32, ctx)
    back_in = sb("back_in", [1, P], F32, ctx)
    link = sb("link", [1, P], F32, ctx)
    again = sb("again", [1, HEADS + 1], F32, ctx)
    again_all = sb("again_all", [P, HEADS + 1], F32, ctx)
    is_node = sb("is_node", [P, BLOCKS], F32, ctx)
    factor = sb("factor", [P, BLOCKS, HEADS], F32, ctx)

    s_staged = sem("s_staged")
    s_pool = sem("s_pool")
    s_sp, s_pe = sem("s_sp"), sem("s_pe")
    s_gath = [sem(f"s_gath{k}") for k in range(U)]
    s_store = [sem(f"s_store{k}") for k in range(U)]
    s_load = [sem(f"s_load{k}") for k in range(V)]
    s_hot = sem("s_hot")
    s_hot_ps = sem("s_hot_ps")
    s_hot_t = sem("s_hot_t")
    s_left = sem("s_left")
    s_z, s_leaky, s_weighed = sem("s_z"), sem("s_leaky"), sem("s_weighed")
    s_score = sem("s_score")
    s_dve_wait = sem("s_dve_wait")
    s_terms = sem("s_terms")
    s_sum_ps = sem("s_sum_ps")
    s_acc = sem("s_acc")
    s_chain = sem("s_att_dve")
    s_sorted_scores, s_sorted_pens = sem("s_sorted_scores"), sem("s_sorted_pens")
    s_fill = sem("s_fill")
    s_score_s, s_pen_s = sem("s_score_s"), sem("s_pen_s")
    s_edge, s_edge_ps = sem("s_edge"), sem("s_edge_ps")
    s_arg, s_exp = sem("s_arg"), sem("s_exp")
    s_again_arg, s_again = sem("s_again_arg"), sem("s_again")
    s_back = sem("s_back")
    s_weights_act, s_weights_dve = sem("s_weights_act"), sem("s_weights_dve")

    SCAN_LINKS = 30
    fills = [(g, min(4, ROW_TILES - g)) for g in range(0, ROW_TILES, 4)]
    n_fills = len(fills)
    act_fills = (n_fills + 1) // 2

    def turned_before(c):
        return 6 * c - 2

    class Part:

        def __init__(self, c):
            known = isinstance(c, int)
            self.c = c
            self.score = not known or c < CHUNKS
            self.sum = not known or c >= 1
            self.turned = 0 if known and c == 0 else turned_before(c)

    def loop(eng, part, body):
        body(part, part.c * steps, True)
        with eng.Fori(part.c * steps + 1, part.c * steps + steps) as j:
            body(part, j, False)

    def walk(eng, turn):
        for c in range(2):
            turn(Part(c))
        with eng.Fori(2, CHUNKS) as c:
            turn(Part(c))
        turn(Part(CHUNKS))

    def score_group(j, k):
        return U * j + k

    def sum_group(j, k):
        return U * j + k - CHUNK_GROUPS

    with nc.Block() as block:
        @block.gpsimd
        def _(pool):
            def body(j):
                for k in range(U):
                    q = score_group(j, k)
                    at_least(pool, s_store[k], j * 16)
                    at_least(pool, s_z, q - U + 1)
                    pool.wait_ge(s_staged, q + 1)
                    pool.sem_inc(s_pool, 1)
                    for g in range(GROUP_TILES):
                        pool.indirect_dma_start(rows[k][:, g, :], None, m.gr_table[:, :],
                                                bass.IndirectOffsetOnAxis(stage[k][:, g:g + 1], 0)).then_inc(s_gath[k], 16)
            body(0)
            with pool.Fori(1, CHUNKS * steps) as j:
                body(j)

        @block.sync
        def _(sp):
            def body(part, j, first):
                for k in range(U):
                    if part.sum:
                        at_least(sp, s_terms, sum_group(j, k) - V + 1)
                        sp.dma_start(rows2[k % V][:, :, :].rearrange("p g f -> p (g f)"),
                                     m.gr_rows[bass.ds(sum_group(j, k), 1), :, :].rearrange("q p f -> p (q f)")
                                     ).then_inc(s_load[k % V], 16)
                    if part.score:
                        sp.wait_ge(s_gath[k], (j + 1) * 16 * GROUP_TILES)
                        sp.dma_start(m.gr_rows[bass.ds(score_group(j, k), 1), :, :].rearrange("q p f -> p (q f)"),
                                     rows[k][:, :, :].rearrange("p g f -> p (g f)")).then_inc(s_store[k], 16)

            def turn(part):
                loop(sp, part, body)
                if part.score:
                    for k in range(U):
                        sp.wait_ge(s_store[k], (part.c * steps + steps) * 16)
                    sp.sem_inc(s_sp, 1)
            walk(sp, turn)

        @block.tensor
        def _(pe):
            def body(part, j, first):
                for k in range(U):
                    q, r = score_group(j, k), sum_group(j, k)
                    if part.score:
                        turn_hot(q + 2, k % 2)
                    if part.sum:
                        pe.wait_ge(s_terms, r + 1)
                        at_least(pe, s_acc, r - 1)
                        for g in range(GROUP_TILES):
                            last = pe.matmul(bank[4 + k % 2][:, 0:HEADS * ACCW], hot2[k % 2][:, g, :],
                                             terms[k % 2][:, g * HEADS:(g + 1) * HEADS, :].rearrange("p h w -> p (h w)"),
                                             start=g == 0, stop=g == GROUP_TILES - 1)
                        last.then_inc(s_sum_ps, 1)
                    if part.score:
                        left(q + 2, k % 2)

            def left(q, slot):
                blk = pe.value_load(m.blk_i[0:1, bass.ds(q, 1)], min_val=0, max_val=BLOCKS - 1)
                pe.wait_ge(s_hot_t, q + 1)
                at_least(pe, s_z, q - 1)
                for g in range(GROUP_TILES):
                    for part in range(3):
                        last = pe.matmul(bank[2 + slot][:, g * D:(g + 1) * D], hot_t[slot][:, g * P:(g + 1) * P],
                                         m.gl_parts[:, bass.ds(blk, 1), part * D:(part + 1) * D].rearrange("p b f -> p (b f)"),
                                         start=part == 0, stop=part == 2)
                last.then_inc(s_left, 1)

            def turn_hot(q, slot):
                pe.wait_ge(s_hot, q + 1)
                at_least(pe, s_hot_t, q - 1)
                turned = bank[slot][:, :].bitcast(BF16)
                for g in range(GROUP_TILES):
                    last = pe.transpose(turned[:, g * P:(g + 1) * P], hot[slot][:, g, :], m.ident_bf[:, :])
                last.then_inc(s_hot_ps, 1)

            def scan(part):
                c = part.c
                e = part.turned + (c - 1 if part.sum else 0)
                pe.wait_ge(s_sorted_scores, c + 1)
                pe.wait_ge(s_sorted_pens, c + 1)
                for j, (g0, n) in enumerate(fills):
                    if j:
                        pe.wait_ge(s_score_s, c * n_fills + j)
                        pe.wait_ge(s_pen_s, c * n_fills + j)
                    for g in range(n):
                        last = pe.transpose(bank[6][:, g * P:(g + 1) * P], top[:, (g0 + g) * P:(g0 + g + 1) * P],
                                            m.ident[:, :])
                    last.then_inc(s_fill, 1)
                    pens = bank[7][:, :].bitcast(BF16)
                    for g in range(n):
                        last = pe.transpose(pens[:, g * P:(g + 1) * P], pen_cols[:, (g0 + g) * P:(g0 + g + 1) * P],
                                            m.ident_bf[:, :])
                    last.then_inc(s_fill, 1)
                pe.wait_ge(s_score_s, (c + 1) * n_fills)
                pe.wait_ge(s_pen_s, (c + 1) * n_fills)
                pe.wait_ge(s_edge, e + 1)
                for v in range(3):
                    last = pe.transpose(bank[6][0:1, v * P:(v + 1) * P], edge_cols[:, v:v + 1], m.ident[:, :])
                last.then_inc(s_edge_ps, 1)
                pe.wait_ge(s_edge, e + 2)
                pe.sem_inc(s_pe, 1)
                pe.transpose(bank[7][:, 0:1], ahead[0:1, 0:P], m.ident[0:1, 0:1]).then_inc(s_edge_ps, 1)
                pe.wait_ge(s_edge, e + 3)
                pe.transpose(bank[6][0:1, 0:P], edge_cols[:, 3:4], m.ident[:, :]).then_inc(s_edge_ps, 1)
                pe.wait_ge(s_edge, e + 4)
                pe.sem_inc(s_pe, 1)
                pe.transpose(bank[7][:, 0:1], back_in[0:1, :], m.ident[0:1, 0:1]).then_inc(s_edge_ps, 1)
                if part.sum:
                    pe.wait_ge(s_edge, e + 5)
                    pe.transpose(bank[6][0:1, 0:P], edge_cols[:, 3:4], m.ident[:, :]).then_inc(s_edge_ps, 1)
                    pe.wait_ge(s_edge, e + 6)
                    pe.wait_ge(s_again, c)
                    pe.matmul(bank[7][:, 0:HEADS + 1], m.ones[0:1, :], again[:, :], start=True, stop=True
                              ).then_inc(s_edge_ps, 1)
                    pe.wait_ge(s_edge, turned_before(c + 1) + c)
                pe.wait_ge(s_exp, c + 1)
                for j, (g0, n) in enumerate(fills):
                    if j >= 2:
                        if j % 2:
                            pe.wait_ge(s_weights_dve, c * (n_fills - act_fills) + j // 2)
                        else:
                            pe.wait_ge(s_weights_act, c * act_fills + j // 2)
                    for g in range(n):
                        last = pe.transpose(bank[6 + j % 2][:, g * P:(g + 1) * P],
                                            score_s[:, (g0 + g) * P:(g0 + g + 1) * P], m.ident[:, :])
                    last.then_inc(s_back, 1)

            for q in range(2):
                turn_hot(q, q)
                left(q, q)

            def turn(part):
                loop(pe, part, body)
                if part.score:
                    scan(part)
            walk(pe, turn)

        def weights_by_tile(g0, n):
            return weights[:, :, :].rearrange("p (r g) h -> p g r h", g=ROW_TILES)[:, g0:g0 + n]

        @block.scalar
        def _(act):
            def move_hot(q, slot):
                at_least(act, s_left, q - 1)
                act.wait_ge(s_hot_ps, q + 1)
                nc.scalar.copy(hot_t[slot][:, :], bank[slot][:, :].bitcast(BF16)[:, 0:GROUP_TILES * P]
                               ).then_inc(s_hot_t, 1)

            def body(part, j, first):
                for k in range(U):
                    move_hot(score_group(j, k) + 2, k % 2)

            for q in range(2):
                move_hot(q, q)

            def turn(part):
                c = part.c
                if not part.score:
                    return
                loop(act, part, body)
                act.wait_ge(s_score, (c + 1) * CHUNK_GROUPS)
                nc.scalar.copy(top[:, :].rearrange("p (g r h) -> p g r h", g=ROW_TILES, h=HEADS),
                               scores[:, :, :].rearrange("p (r g) h -> p g r h", g=ROW_TILES)
                               ).then_inc(s_sorted_scores, 1)
                for j, (g0, n) in enumerate(fills):
                    act.wait_ge(s_fill, 2 * (c * n_fills + j) + 1)
                    nc.scalar.copy(score_s[:, g0 * P:(g0 + n) * P], bank[6][:, 0:n * P]).then_inc(s_score_s, 1)
                if part.sum:
                    act.wait_ge(s_again_arg, c)
                    nc.scalar.activation(again[:, 0:HEADS], again[:, 0:HEADS], ACT.Exp).then_inc(s_again, 1)
                act.wait_ge(s_arg, c + 1)
                nc.scalar.activation(score_s[:, :], score_s[:, :], ACT.Exp).then_inc(s_exp, 1)
                for j, (g0, n) in enumerate(fills):
                    if j % 2 == 0:
                        act.wait_ge(s_back, c * n_fills + j + 1)
                        nc.scalar.copy(weights_by_tile(g0, n),
                                       bank[6][:, 0:n * P].rearrange("p (g r h) -> p g r h", g=n, h=HEADS)
                                       ).then_inc(s_weights_act, 1)
            walk(act, turn)

        @block.vector
        def _(dve):
            chain = Chain(dve, s_chain)
            att = m.att[:, :].unsqueeze(1).to_broadcast([P, GROUP_TILES, D])
            places = m.iota_row[:, :].unsqueeze(1).to_broadcast([P, GROUP_TILES, P])

            def hot_of(out, q):
                at = m.place[:, bass.ds(q * GROUP_TILES, GROUP_TILES)].unsqueeze(2).to_broadcast([P, GROUP_TILES, P])
                return dve.tensor_tensor(out[:, :, :], places, at, ALU.is_equal)

            def stage_of(k, q):
                return dve.tensor_scalar(stage[k][:, :], m.row_of[:, bass.ds(q * GROUP_TILES, GROUP_TILES)], 0.0, None,
                                         ALU.add)

            def body(part, j, first):
                for k in range(U):
                    q, r = score_group(j, k), sum_group(j, k)
                    tile = (U * j + k) * GROUP_TILES - part.c * CHUNK_TILES
                    if not isinstance(tile, int):
                        tile = nc.s_assert_within(tile, 0, CHUNK_TILES - GROUP_TILES, skip_runtime_bounds_check_because=
                                                  "a step's groups are its chunk's")
                    if part.score:
                        dve.wait_ge(s_left, q + 1)
                        dve.wait_ge(s_gath[k], (j + 1) * 16 * GROUP_TILES)
                        dve.tensor_tensor(z[:, :, :], bank[2 + k % 2][:, 0:GW].rearrange("p (g f) -> p g f", f=D),
                                          rows[k][:, :, :], ALU.add).then_inc(s_z, 1)
                    if part.sum:
                        at_least(dve, s_sum_ps, r - 1)
                        hot_of(hot2[k % 2], r)
                    if part.score:
                        dve.wait_ge(s_z, q + 1)
                        dve.scalar_tensor_tensor(leaky[:, :, :], z[:, :, :], SLOPE, z[:, :, :], ALU.mult,
                                                 ALU.max).then_inc(s_leaky, 1)
                    if part.sum:
                        weight = weights[:, bass.ds(tile, GROUP_TILES), :].rearrange("p g h -> p (g h)")
                        dve.wait_ge(s_load[k % V], ((j - steps) * (U // V) + k // V + 1) * 16)
                        dve.tensor_tensor(terms[k % 2][:, :, 0:DH],
                                          rows2[k % V][:, :, :].rearrange("p g (h f) -> p (g h) f", f=DH),
                                          weight.unsqueeze(2).to_broadcast([P, PAIRS, DH]), ALU.mult)
                        dve.tensor_copy(terms[k % 2][:, :, DH:ACCW], weight.unsqueeze(2)).then_inc(s_terms, 1)
                    if part.score:
                        dve.wait_ge(s_leaky, q + 1)
                        dve.tensor_tensor(weighed[:, :, :], leaky[:, :, :], att, ALU.mult).then_inc(s_weighed, 1)
                        dve.wait_ge(s_hot_ps, q + 1)
                        hot_of(hot[k % 2], q + 2).then_inc(s_hot, 1)
                        at_least(dve, s_gath[(k - 1) % U], (j + (k > 0)) * 16 * GROUP_TILES)
                        stage_of((k - 1) % U, q + U - 1).then_inc(s_staged, 1)
                        dve.wait_ge(s_weighed, q + 1)
                        dve.sem_inc(s_dve_wait, 1)
                        nc_reduce(dve, scores[:, bass.ds(tile, GROUP_TILES), :].rearrange("p g h -> p (g h)"),
                                  weighed[:, :, :].rearrange("p g (h f) -> p (g h) f", f=DH)).then_inc(s_score, 1)
                    if part.sum and not (first and k == 0):
                        accumulate(r - 1, (k - 1) % 2)

            def accumulate(r, slot):
                blk = dve.value_load(m.blk_i[0:1, bass.ds(r, 1)], min_val=0, max_val=BLOCKS - 1)
                sums = m.acc[:, bass.ds(blk, 1), :].rearrange("p b w -> p (b w)")
                at_least(dve, s_acc, r)
                dve.wait_ge(s_sum_ps, r + 1)
                dve.tensor_tensor(sums, sums, bank[4 + slot][:, 0:HEADS * ACCW], ALU.add).then_inc(s_acc, 1)

            def scan(part):
                c = part.c
                pens = m.pen[:, bass.ds(c * CHUNK_TILES, CHUNK_TILES)].rearrange("p (r g) -> p g r", g=ROW_TILES)
                dve.tensor_copy(pen_cols.rearrange("p (g r h) -> p g r h", g=ROW_TILES, h=HEADS),
                                pens.unsqueeze(3).to_broadcast([P, ROW_TILES, CHUNK_ROWS, HEADS])
                                ).then_inc(s_sorted_pens, 1)
                for j, (g0, n) in enumerate(fills):
                    dve.wait_ge(s_fill, 2 * (c * n_fills + j) + 2)
                    dve.tensor_copy(pen_s[:, g0 * P:(g0 + n) * P], bank[7][:, :].bitcast(BF16)[:, 0:n * P]
                                    ).then_inc(s_pen_s, 1)
                dve.wait_ge(s_pen_s, (c + 1) * n_fills)
                dve.wait_ge(s_score_s, (c + 1) * n_fills)
                down = slice(None, None, -1)
                chain.link(dve.tensor_tensor_scan(top_f[:, :], pen_s[:, 0:SCAN], score_s[:, :], -BIG, ALU.add, ALU.max))
                dve.tensor_copy(edge_cols[:, 0:1], pen_s[:, 0:1])
                nc_reduce(dve, edge_cols[:, 1:2], pen_s[:, 1:SCAN], ALU.min)
                dve.tensor_copy(edge_cols[:, 2:3], top_f[:, SCAN - 1:SCAN]).then_inc(s_edge, 1)
                dve.wait_ge(s_edge_ps, part.turned + 1)
                chain.link(dve.tensor_copy(edge_rows[:, 0:3, :].rearrange("p v q -> p (v q)"), bank[6][0:1, 0:3 * P]))
                chain.link(dve.tensor_tensor(least[:, :], edge_rows[:, 0, :], edge_rows[:, 1, :], ALU.min))
                for h in range(HEADS):
                    chain.link(dve.tensor_tensor_scan(ahead[:, HEADS + h::HEADS], least[:, h::HEADS],
                                                      edge_rows[:, 2, h::HEADS], ahead[:, h:h + 1], ALU.add, ALU.max))
                dve.sem_inc(s_edge, 1)
                dve.wait_ge(s_edge_ps, part.turned + 2)
                chain.link(dve.tensor_copy(init[:, :], bank[7][:, 0:1]))
                chain.link(dve.tensor_tensor_scan(top_f[:, :], pen_s[:, 0:SCAN], score_s[:, :], init[:, :], ALU.add, ALU.max))
                chain.link(dve.tensor_tensor_scan(top[:, down], pen_s[:, 1:SCAN + 1][:, down], top_f[:, down], -BIG,
                                                  ALU.add, ALU.max))
                dve.tensor_copy(edge_cols[:, 3:4], top[:, 0:1]).then_inc(s_edge, 1)
                dve.wait_ge(s_edge_ps, part.turned + 3)
                chain.link(dve.tensor_copy(edge_rows[:, 3, :], bank[6][0:1, 0:P]))
                chain.link(dve.tensor_tensor(link[:, 0:P - HEADS], edge_rows[:, 0, HEADS:P], edge_rows[:, 1, 0:P - HEADS],
                                             ALU.add))
                for h in range(HEADS):
                    chain.link(dve.tensor_tensor_scan(back[:, h:P:HEADS][:, down], link[:, h::HEADS][:, down],
                                                      edge_rows[:, 3, h::HEADS][:, down], back[:, P + h:P + h + 1],
                                                      ALU.add, ALU.max))
                dve.tensor_tensor(back_in[:, 0:P - HEADS], back[:, HEADS:P], edge_rows[:, 0, HEADS:P], ALU.add
                                  ).then_inc(s_edge, 1)
                dve.wait_ge(s_edge_ps, part.turned + 4)
                chain.link(dve.tensor_copy(init[:, :], bank[7][:, 0:1]))
                chain.link(dve.tensor_tensor_scan(top[:, down], pen_s[:, 1:SCAN + 1][:, down], top_f[:, down], init[:, :],
                                                  ALU.add, ALU.max))
                if part.sum:
                    dve.tensor_copy(edge_cols[:, 3:4], top[:, 0:1]).then_inc(s_edge, 1)
                    dve.wait_ge(s_edge_ps, part.turned + 5)
                    chain.link(dve.tensor_copy(edge_rows[:, 3, :], bank[6][0:1, 0:P]))
                    chain.link(dve.tensor_tensor(again[:, 0:HEADS], ahead[:, 0:HEADS], edge_rows[:, 3, 0:HEADS],
                                                 ALU.subtract))
                    chain.link(dve.tensor_scalar(link[:, 0:HEADS], edge_rows[:, 0, 0:HEADS], 0.0, None, ALU.is_equal))
                    dve.tensor_tensor(again[:, 0:HEADS], again[:, 0:HEADS], link[:, 0:HEADS], ALU.mult
                                      ).then_inc(s_again_arg, 1)
                dve.tensor_tensor(score_s[:, :], score_s[:, :], top[:, :], ALU.subtract).then_inc(s_arg, 1)
                if part.sum:
                    dve.scalar_tensor_tensor(again[:, HEADS:HEADS + 1], m.blk_f[:, bass.ds(c * CHUNK_GROUPS, 1)], float(P),
                                             m.place[0:1, bass.ds(c * CHUNK_TILES, 1)], ALU.mult, ALU.add).then_inc(s_edge, 1)
                    dve.wait_ge(s_edge_ps, part.turned + 6)
                    chain.link(dve.tensor_copy(again_all[:, :], bank[7][:, 0:HEADS + 1]))
                    dve.sem_inc(s_edge, 1)
                    chain.link(dve.tensor_scalar(is_node[:, :], m.iota_node[:, :], again_all[:, HEADS:HEADS + 1], None,
                                                 ALU.is_equal))
                    chain.link(dve.tensor_scalar(again_all[:, 0:HEADS], again_all[:, 0:HEADS], -1.0, None, ALU.add))
                    for h in range(HEADS):
                        chain.link(dve.tensor_scalar(factor[:, :, h], is_node[:, :], again_all[:, h:h + 1], 1.0, ALU.mult,
                                                     ALU.add))
                    by_head = m.acc[:, :, :].rearrange("p b (h w) -> p (b h) w", w=ACCW)
                    chain.link(dve.tensor_tensor(by_head, by_head, factor[:, :, :].rearrange("p b h -> p (b h)").unsqueeze(2)
                                                 .to_broadcast([P, BLOCKS * HEADS, ACCW]), ALU.mult))
                chain.link(dve.tensor_copy(ahead[:, 0:HEADS], ahead[:, P:P + HEADS]))
                for j, (g0, n) in enumerate(fills):
                    if j % 2:
                        dve.wait_ge(s_back, c * n_fills + j + 1)
                        dve.tensor_copy(weights_by_tile(g0, n),
                                        bank[7][:, 0:n * P].rearrange("p (g r h) -> p g r h", g=n, h=HEADS)
                                        ).then_inc(s_weights_dve, 1)
                dve.wait_ge(s_weights_dve, (c + 1) * (n_fills - act_fills))
                dve.wait_ge(s_weights_act, (c + 1) * act_fills)

            for k in range(U - 1):
                stage_of(k, k).then_inc(s_staged, 1)
            chain.link(dve.memset(m.acc[:, :, :], 0.0))
            dve.memset(pen_s[:, SCAN:SCAN + 1], 0.0)
            dve.memset(ahead[:, :], -BIG)
            dve.memset(back[:, :], -BIG)
            dve.memset(back_in[:, :], -BIG)
            chain.link(dve.memset(link[:, :], -BIG))
            for q in range(2):
                hot_of(hot[q], q).then_inc(s_hot, 1)

            def turn(part):
                loop(dve, part, body)
                if part.sum:
                    accumulate(part.c * CHUNK_GROUPS - 1, (U - 1) % 2)
                    dve.wait_ge(s_acc, part.c * CHUNK_GROUPS)
                if part.score:
                    before = chain.n
                    if not isinstance(part.c, int):
                        chain.turns = (part.c - 2) * SCAN_LINKS
                    scan(part)
                    if part.sum:
                        assert chain.n - before == SCAN_LINKS, chain.n - before
            walk(dve, turn)


def attention_nodes(m, ctx):
    nc, sb, sem, bank = m.nc, m.sb, m.sem, m.bank
    share = sb("share", [P, BLOCKS * HEADS], F32, ctx)
    mixed = sb("mixed", [P, BLOCKS, D], F32, ctx)
    mixed_t = [sb(f"mixed_t{i}", [D, 512], F32, ctx) for i in range(2)]
    normed_t = [sb(f"normed_t{i}", [D, 512], F32, ctx) for i in range(2)]
    hidden_t = [sb(f"hidden_t{i}", [D, 512], F32, ctx) for i in range(2)]
    s_x = sem("s_x_again")
    s_preset = sem("s_x_preset")
    s_layer1 = sem("s_layer1")
    s_chain = sem("s_nodes0_dve")
    s_mixed = sem("s_mixed")
    s_in_ps, s_in = sem("s_in_ps"), sem("s_in")
    s_hid_ps, s_hid = sem("s_hid_ps"), sem("s_hid")
    s_out_ps, s_add = sem("s_out_ps"), sem("s_add")
    s_var, s_std = sem("s_var1"), sem("s_std1")
    s_h2, s_stored = sem("s_h2"), sem("s_h2_stored")
    rounds = [(b, min(4, BLOCKS - b)) for b in range(0, BLOCKS, 4)]

    with nc.Block() as block:
        @block.gpsimd
        def _(pool):
            pool.iota(m.nodes[:, :], [[1, BLOCKS * P]], base=0, channel_multiplier=0,
                      allow_small_or_imprecise_dtypes=True).then_inc(s_layer1, 1)
            pool.memset(m.agg[:, :, :], 0.0).then_inc(s_layer1, 1)
            pool.tensor_copy(m.dst_f[:, :], m.dst[:, :]).then_inc(s_layer1, 1)
            pool.wait_ge(s_layer1, 3)

        @block.sync
        def _(sp):
            sp.wait_ge(s_preset, 1)
            load_blocks(sp, m.x, m.t["x"], s_x)
            sp.wait_ge(s_h2, 1)
            store_blocks(sp, m.h2_table, m.h, s_stored)
            sp.wait_ge(s_stored, 32)

        @block.tensor
        def _(pe):
            def turned(r):
                b, n = rounds[r]
                if r >= 2:
                    pe.wait_ge(s_in, 2 * r - 2)
                for i in range(n):
                    pe.transpose(bank[r % 2][0:D, i * P:(i + 1) * P], mixed[:, b + i, :], m.ident[:, :])
                    last = pe.transpose(bank[6 + r % 2][0:D, i * P:(i + 1) * P], m.h[:, b + i, :], m.ident[:, :])
                last.then_inc(s_in_ps, 1)

            def hidden(r):
                n = rounds[r][1]
                pe.wait_ge(s_in, 2 * r + 2)
                if r >= 2:
                    pe.wait_ge(s_hid, r - 1)
                hid = bank[2 + r % 2][0:D, 0:n * P]
                pe.matmul(hid, m.w1t_out[:, :], mixed_t[r % 2][:, 0:n * P], start=True, stop=False)
                pe.matmul(hid, m.w1t_h[:, :], normed_t[r % 2][:, 0:n * P], start=False, stop=True).then_inc(s_hid_ps, 1)

            def output(r):
                n = rounds[r][1]
                pe.wait_ge(s_hid, r + 1)
                if r >= 2:
                    pe.wait_ge(s_add, r - 1)
                for i in range(n):
                    last = pe.matmul(bank[4 + r % 2][:, i * D:(i + 1) * D], hidden_t[r % 2][:, i * P:(i + 1) * P],
                                     m.w2t[:, :], start=True, stop=True)
                last.then_inc(s_out_ps, 1)

            pe.wait_ge(s_mixed, 1)
            for r in range(len(rounds) + 2):
                if r < len(rounds):
                    turned(r)
                if 1 <= r <= len(rounds):
                    hidden(r - 1)
                if r >= 2:
                    output(r - 2)

        @block.scalar
        def _(act):
            def move(r):
                n = rounds[r][1]
                if r >= 2:
                    act.wait_ge(s_hid_ps, r - 1)
                act.wait_ge(s_in_ps, r + 1)
                nc.scalar.copy(mixed_t[r % 2][:, 0:n * P], bank[r % 2][0:D, 0:n * P]).then_inc(s_in, 1)
                nc.scalar.copy(normed_t[r % 2][:, 0:n * P], bank[6 + r % 2][0:D, 0:n * P]).then_inc(s_in, 1)

            def gelu(r):
                n = rounds[r][1]
                act.wait_ge(s_hid_ps, r + 1)
                if r >= 2:
                    act.wait_ge(s_out_ps, r - 1)
                nc.scalar.activation(hidden_t[r % 2][:, 0:n * P], bank[2 + r % 2][0:D, 0:n * P], ACT.Gelu,
                                     bias=m.b1_l0[:, :]).then_inc(s_hid, 1)

            for r in range(len(rounds) + 1):
                if r < len(rounds):
                    move(r)
                if r >= 1:
                    gelu(r - 1)
            act.wait_ge(s_var, 1)
            nc.scalar.activation(m.rstd[:, :], m.var[:, :], ACT.Sqrt).then_inc(s_std, 1)

        @block.vector
        def _(dve):
            chain = Chain(dve, s_chain)
            by_head = m.acc[:, :, :].rearrange("p b (h w) -> p (b h) w", w=ACCW)
            dve.memset(m.x[:, BLOCKS - 1, :], 0.0).then_inc(s_preset, 1)
            chain.link(dve.tensor_scalar(share[:, :].unsqueeze(2), by_head[:, :, DH:ACCW], 1e-16, None, ALU.add))
            chain.link(dve.reciprocal(share[:, :], share[:, :]))
            dve.tensor_tensor(mixed[:, :, :].rearrange("p b (h f) -> p (b h) f", f=DH), by_head[:, :, 0:DH],
                              share[:, :].unsqueeze(2).to_broadcast([P, BLOCKS * HEADS, DH]), ALU.mult
                              ).then_inc(s_mixed, 1)
            dve.wait_ge(s_x, 32)
            chain.link(dve.tensor_tensor(m.x[:, :, :], m.x[:, :, :],
                                         m.b2_l0[:, :].unsqueeze(1).to_broadcast([P, BLOCKS, D]), ALU.add))
            for r, (b, n) in enumerate(rounds):
                dve.wait_ge(s_out_ps, r + 1)
                dve.tensor_tensor(m.x[:, b:b + n, :], m.x[:, b:b + n, :],
                                  bank[4 + r % 2][:, 0:n * D].rearrange("p (b f) -> p b f", f=D), ALU.add
                                  ).then_inc(s_add, 1)
            dve.wait_ge(s_add, len(rounds))
            layernorm_steps(m, chain, dve, m.x, m.h, mixed, s_var, s_std, 1).then_inc(s_h2, 1)


def messages(m, ctx):
    nc, sb, sem, bank = m.nc, m.sb, m.sem, m.bank
    attrs = m.t["edge_attr_64"]
    U = 4
    rows = [sb(f"message{k}", [P, EDGE_TILES, D], F32, ctx) for k in range(U)]
    edge = [sb(f"edge{k}", [P, EDGE_TILES, D], F32, ctx) for k in range(U)]
    stage = [sb(f"edge_stage{k}", [P, EDGE_TILES], I32, ctx) for k in range(U)]
    hot = [sb(f"edge_hot{k}", [P, EDGE_TILES, P], F32, ctx) for k in range(2)]
    hot_more = sb("edge_hot_more", [P, EDGE_TILES, P], F32, ctx)
    s_staged, s_pool = sem("s_edge_staged"), sem("s_edge_pool")
    s_gath = [sem(f"s_edge_gath{k}") for k in range(U)]
    s_edge = [sem(f"s_edge{k}") for k in range(U)]
    s_message = sem("s_message")
    s_first_ps = sem("s_edge_first_ps")
    s_hot = sem("s_edge_hot")
    s_sum_ps = sem("s_edge_sum_ps")
    s_agg = sem("s_agg")
    s_done = sem("s_done")
    assert EDGE_GROUPS % U == 0
    last_i = EDGE_GROUPS // U - 1

    def loop(eng, body):
        body(0)
        with eng.Fori(1, last_i) as i:
            body(i)
        body(last_i)

    def steps_before(eng, g):
        return eng.value_load(m.step_of[0:1, bass.ds(g, 1)], min_val=0, max_val=BLOCKS * EDGE_GROUPS)

    with nc.Block() as block:
        @block.gpsimd
        def _(pool):
            def body(i):
                for k in range(U):
                    g = U * i + k
                    at_least(pool, s_first_ps, g - U + 1)
                    at_least(pool, s_done, g - U + 1)
                    pool.wait_ge(s_staged, g + 1)
                    pool.sem_inc(s_pool, 1)
                    for e in range(EDGE_TILES):
                        pool.indirect_dma_start(rows[k][:, e, :], None, m.h2_table[:, :],
                                                bass.IndirectOffsetOnAxis(stage[k][:, e:e + 1], 0)).then_inc(s_gath[k], 16)
            loop(pool, body)

        @block.sync
        def _(sp):
            full = attrs[0:FULL_EDGES, :].rearrange("(g p t) f -> g p (t f)", p=P, t=EDGE_TILES)
            tail = attrs[FULL_EDGES:E, :].rearrange("(p t) f -> p (t f)", t=EDGE_TILES)

            def body(i):
                for k in range(U):
                    g = U * i + k
                    at_least(sp, s_message, g - U + 1)
                    if isinstance(g, int) and g == EDGE_GROUPS - 1:
                        sp.dma_start(edge[k][0:TAIL_PARTS, :, :].rearrange("p t f -> p (t f)"), tail).then_inc(s_edge[k], 16)
                    else:
                        sp.dma_start(edge[k][:, :, :].rearrange("p t f -> p (t f)"),
                                     full[bass.ds(g, 1), :, :].rearrange("g p f -> p (g f)")).then_inc(s_edge[k], 16)
            loop(sp, body)

        @block.tensor
        def _(pe):
            def body(i):
                for k in range(U):
                    g = U * i + k
                    pe.wait_ge(s_message, g + 1)
                    for e in range(EDGE_TILES):
                        last = pe.matmul(bank[k % 2][:, 0:D], hot[k % 2][:, e, :], rows[k][:, e, :], start=e == 0,
                                         stop=e == EDGE_TILES - 1)
                    last.then_inc(s_first_ps, 1)
                    before, end = steps_before(pe, g), steps_before(pe, g + 1)
                    with pe.If_lt(pe.to_reg(before), pe.to_reg(end)), pe.Fori(before, end) as r:
                        pe.wait_ge(s_hot, r + 1)
                        for e in range(EDGE_TILES):
                            last = pe.matmul(bank[2][:, 0:D], hot_more[:, e, :], rows[k][:, e, :], start=e == 0,
                                             stop=e == EDGE_TILES - 1)
                        last.then_inc(s_sum_ps, 1)
            loop(pe, body)

        @block.vector
        def _(dve):
            def stage_of(k, g):
                return dve.tensor_scalar(stage[k][:, :], m.src[:, bass.ds(g * EDGE_TILES, EDGE_TILES)], 0.0, None, ALU.add)

            def hot_of(out, g, blk):
                to = m.dst_f[:, bass.ds(g * EDGE_TILES, EDGE_TILES)].unsqueeze(2).to_broadcast([P, EDGE_TILES, P])
                return dve.tensor_tensor(out[:, :, :], m.nodes[:, bass.ds(blk * P, P)].unsqueeze(1).to_broadcast(
                    [P, EDGE_TILES, P]), to, ALU.is_equal)

            def add_first(g, k, steps):
                blk = dve.value_load(m.first_of[0:1, bass.ds(g, 1)], min_val=0, max_val=BLOCKS - 1)
                sums = m.agg[:, bass.ds(blk, 1), :].rearrange("p b f -> p (b f)")
                at_least(dve, s_agg, steps + g)
                dve.wait_ge(s_first_ps, g + 1)
                dve.tensor_tensor(sums, sums, bank[k][:, 0:D], ALU.add).then_inc(s_agg, 1)

            def body(i):
                for k in range(U):
                    g = U * i + k
                    if not (isinstance(g, int) and g > EDGE_GROUPS - U):
                        at_least(dve, s_gath[(k - 1) % U], (i + (k > 0)) * 16 * EDGE_TILES)
                        stage_of((k - 1) % U, g + U - 1).then_inc(s_staged, 1)
                    before = steps_before(dve, g)
                    blk = dve.value_load(m.first_of[0:1, bass.ds(g, 1)], min_val=0, max_val=BLOCKS - 1)
                    if not (isinstance(g, int) and g == 0):
                        add_first(g - 1, 1 - k % 2, before)
                    hot_of(hot[k % 2], g, blk)
                    dve.wait_ge(s_edge[k], (i + 1) * 16)
                    dve.wait_ge(s_gath[k], (i + 1) * 16 * EDGE_TILES)
                    dve.tensor_tensor(rows[k][:, :, :], rows[k][:, :, :], edge[k][:, :, :], ALU.add).then_inc(s_message, 1)
                    moved = dve.value_load(m.shift[0:1, bass.ds(g, 1)], min_val=SHIFT - BLOCKS * EDGE_GROUPS,
                                           max_val=SHIFT + BLOCKS)
                    end = steps_before(dve, g + 1)
                    with dve.If_lt(dve.to_reg(before), dve.to_reg(end)), dve.Fori(before, end) as r:
                        blk = nc.s_assert_within(r + moved - SHIFT, 0, BLOCKS - 1, skip_runtime_bounds_check_because=
                                                 "the steps of a group are blocks of its dst")
                        hot_of(hot_more, g, blk).then_inc(s_hot, 1)
                        at_least(dve, s_agg, r + g)
                        dve.wait_ge(s_sum_ps, r + 1)
                        sums = m.agg[:, bass.ds(blk, 1), :].rearrange("p b f -> p (b f)")
                        dve.tensor_tensor(sums, sums, bank[2][:, 0:D], ALU.add).then_inc(s_agg, 1)
                    dve.engine_nop().then_inc(s_done, 1)
            for k in range(U - 1):
                stage_of(k, k).then_inc(s_staged, 1)
            loop(dve, body)
            add_first(EDGE_GROUPS - 1, 1, steps_before(dve, EDGE_GROUPS))



def message_nodes(m, ctx):
    nc, sb, sem, bank = m.nc, m.sb, m.sem, m.bank
    agg_t = [sb(f"agg_t{i}", [D, 512], F32, ctx) for i in range(2)]
    hidden_t = [sb(f"wide_t{i}", [2 * D, 512], F32, ctx) for i in range(2)]
    y = sb("y", [D, BLOCKS * P], F32, ctx)
    square = sb("y_square", [D, N], F32, ctx)
    stats = sb("stats", [D, 4], F32, ctx)
    s_chain = sem("s_nodes1_dve")
    s_in_ps, s_in = sem("s_agg_ps"), sem("s_agg_t")
    s_hid_ps, s_hid = sem("s_wide_ps"), sem("s_wide")
    s_y_ps, s_y = sem("s_y_ps"), sem("s_y")
    s_var, s_std = sem("s_var2"), sem("s_std2")
    s_mean, s_square = sem("s_mean"), sem("s_square")
    s_norm = sem("s_norm")
    s_back, s_add = sem("s_y_back"), sem("s_result")
    s_out = sem("s_out")
    rounds = [(b, min(4, BLOCKS - b)) for b in range(0, BLOCKS, 4)]
    part = sb("part_sums", [D, len(rounds)], F32, ctx)
    turns = [(b, min(8, BLOCKS - b)) for b in range(0, BLOCKS, 8)]

    with nc.Block() as block:
        @block.tensor
        def _(pe):
            def turned(r):
                b, n = rounds[r]
                if r >= 2:
                    pe.wait_ge(s_in, r - 1)
                for i in range(n):
                    last = pe.transpose(bank[r % 2][0:D, i * P:(i + 1) * P], m.agg[:, b + i, :], m.ident[:, :])
                last.then_inc(s_in_ps, 1)

            def hidden(r):
                n = rounds[r][1]
                pe.wait_ge(s_in, r + 1)
                if r >= 2:
                    pe.wait_ge(s_hid, r - 1)
                pe.matmul(bank[2 + r % 2][:, 0:n * P], m.w1_l1[:, :], agg_t[r % 2][:, 0:n * P], start=True, stop=True
                          ).then_inc(s_hid_ps, 1)

            def output(r):
                n = rounds[r][1]
                pe.wait_ge(s_hid, r + 1)
                if r >= 2:
                    pe.wait_ge(s_y, r - 1)
                pe.matmul(bank[4 + r % 2][0:D, 0:n * P], m.w2_l1[:, :], hidden_t[r % 2][:, 0:n * P], start=True,
                          stop=True).then_inc(s_y_ps, 1)

            for r in range(len(rounds) + 2):
                if r < len(rounds):
                    turned(r)
                if 1 <= r <= len(rounds):
                    hidden(r - 1)
                if r >= 2:
                    output(r - 2)
            pe.wait_ge(s_norm, 1)
            for r, (b, n) in enumerate(turns):
                if r >= 2:
                    pe.wait_ge(s_add, r - 1)
                for i in range(n):
                    last = pe.transpose(bank[6 + r % 2][:, i * D:(i + 1) * D], y[:, (b + i) * P:(b + i + 1) * P],
                                        m.ident[0:D, 0:D])
                last.then_inc(s_back, 1)

        @block.scalar
        def _(act):
            def move(r):
                n = rounds[r][1]
                if r >= 2:
                    act.wait_ge(s_hid_ps, r - 1)
                act.wait_ge(s_in_ps, r + 1)
                nc.scalar.copy(agg_t[r % 2][:, 0:n * P], bank[r % 2][0:D, 0:n * P]).then_inc(s_in, 1)

            def result(r):
                b, n = rounds[r]
                act.wait_ge(s_y_ps, r + 1)
                cols = slice(b * P, min((b + n) * P, N))
                nc.scalar.activation(y[:, cols], bank[4 + r % 2][0:D, 0:cols.stop - cols.start], ACT.Identity,
                                     bias=m.cols_l1[:, 0:1], accum_out=part[:, r:r + 1]).then_inc(s_y, 1)

            for r in range(len(rounds) + 2):
                if r < len(rounds):
                    move(r)
                if r >= 2:
                    result(r - 2)
            act.wait_ge(s_mean, 1)
            nc.scalar.activation(square[:, :], y[:, 0:N], ACT.Square, bias=stats[:, 0:1], accum_out=stats[:, 1:2]
                                 ).then_inc(s_square, 1)
            act.wait_ge(s_var, 1)
            nc.scalar.activation(stats[:, 2:3], stats[:, 1:2], ACT.Sqrt).then_inc(s_std, 1)

        @block.vector
        def _(dve):
            c = Chain(dve, s_chain)
            dve.memset(y[:, N:], 0.0)
            for r, (b, n) in enumerate(rounds):
                dve.wait_ge(s_hid_ps, r + 1)
                if r >= 2:
                    dve.wait_ge(s_y_ps, r - 1)
                dve.tensor_scalar(hidden_t[r % 2][:, 0:n * P], bank[2 + r % 2][:, 0:n * P], m.b1_l1[:, :], 0.0,
                                  ALU.add, ALU.max).then_inc(s_hid, 1)
            dve.wait_ge(s_y, len(rounds))
            c.link(nc_reduce(dve, stats[:, 0:1], part[:, :]))
            c.link(dve.tensor_scalar(stats[:, 0:1], stats[:, 0:1], -1.0 / N, None, ALU.mult))
            dve.engine_nop().then_inc(s_mean, 1)
            dve.wait_ge(s_square, 1)
            dve.tensor_scalar(stats[:, 1:2], stats[:, 1:2], 1.0 / N, BN_EPS, ALU.mult, ALU.add).then_inc(s_var, 1)
            dve.wait_ge(s_std, 1)
            c.link(dve.reciprocal(stats[:, 2:3], stats[:, 2:3]))
            c.link(dve.tensor_tensor(stats[:, 3:4], stats[:, 2:3], stats[:, 2:3], ALU.mult))
            c.link(dve.tensor_tensor(stats[:, 3:4], stats[:, 3:4], stats[:, 1:2], ALU.mult))
            c.link(dve.tensor_scalar(stats[:, 3:4], stats[:, 3:4], -0.5, 1.5, ALU.mult, ALU.add))
            c.link(dve.tensor_tensor(stats[:, 2:3], stats[:, 2:3], stats[:, 3:4], ALU.mult))
            c.link(dve.tensor_tensor(stats[:, 2:3], stats[:, 2:3], m.cols_l1[:, 1:2], ALU.mult))
            c.link(dve.scalar_tensor_tensor(stats[:, 3:4], stats[:, 0:1], stats[:, 2:3], m.cols_l1[:, 2:3], ALU.mult,
                                            ALU.add))
            dve.tensor_scalar(y[:, :], y[:, :], stats[:, 2:3], stats[:, 3:4], ALU.mult, ALU.add).then_inc(s_norm, 1)
            for r, (b, n) in enumerate(turns):
                dve.wait_ge(s_back, r + 1)
                dve.tensor_tensor(m.x[:, b:b + n, :], m.x[:, b:b + n, :],
                                  bank[6 + r % 2][:, 0:n * D].rearrange("p (b f) -> p b f", f=D), ALU.add
                                  ).then_inc(s_add, 1)

        @block.sync
        def _(sp):
            sp.wait_ge(s_add, len(turns))
            store_blocks(sp, m.out, m.x, s_out)
            sp.wait_ge(s_out, 32)


_INS = ['x', 'src', 'dst', 'edge_attr_64', 'L0_gnn_Wl', 'L0_gnn_Wr', 'L0_gnn_att', 'L0_gnn_W1', 'L0_gnn_b1',
        'L0_gnn_W2', 'L0_gnn_b2', 'L1_gnn_W1', 'L1_gnn_b1', 'L1_gnn_W2', 'L1_gnn_b2', 'L1_gnn_bn_gamma',
        'L1_gnn_bn_beta']


def kernel(**inputs):
    import concourse.bacc as bacc
    from concourse.bass_utils import run_bass_kernel_spmd

    nc = bacc.Bacc("TRN2", target_bir_lowering=False, num_devices=1)
    arrays, t = {}, {}
    for name in _INS:
        a = np.ascontiguousarray(inputs[name])
        arrays[f"in_{name}"] = a
        t[name] = nc.dram_tensor(f"in_{name}", a.shape, mybir.dt.from_np(a.dtype), kind="ExternalInput").ap()
    out = nc.dram_tensor("out_0", (N, D), F32, kind="ExternalOutput").ap()
    build(nc, t, out)
    r = run_bass_kernel_spmd(nc, [arrays], core_ids=[0])
    return r.results[0]["out_0"]
```
